# Optimizing a Trainium2 kernel written in Bass

```python
import numpy as np
import jax
import jax.numpy as jnp

def _softmax(x, axis=-1):
    return jax.nn.softmax(x, axis=axis)

def _gelu(x):
    return jax.nn.gelu(x, approximate=True)

def _silu(x):
    return jax.nn.silu(x)

def _sigmoid(x):
    return jax.nn.sigmoid(x)

def _layernorm(x, axis=-1, eps=1e-05):
    m = jnp.mean(x, axis=axis, keepdims=True)
    v = jnp.var(x, axis=axis, keepdims=True)
    return (x - m) / jnp.sqrt(v + eps)

def _scatter_add(tgt, idx, src, axis=0):
    return tgt.at[idx].add(src)

def _segment_sum(src, seg, n):
    return jax.ops.segment_sum(src, seg, n)
kernel_name = 'mk_audio_tower_d1_tok_audfeat1024_r4_a7b1eb'

def setup_inputs(seed: int=0):
    np.random.seed(seed)
    _w = jnp.asarray

    def _rec_inputs():
        import jax
        import jax.numpy as jnp
        _rk = jax.random.key(seed)
        x = -0.000125008 + 0.999885 * jax.random.normal(jax.random.fold_in(_rk, 1), (8, 750, 256), jnp.float32)
        return x
    x = _rec_inputs()

    def _L0_tok_setup():
        import jax, jax.numpy as jnp
        import numpy as np
        H = 32
        DECAY = 0.9
        key = jax.random.key(seed)
        ks = jax.random.split(key, 6)
        B, T, D = (8, 1024, 256)
        x = jax.random.normal(ks[0], (B, T, D), dtype=jnp.float32)
        s = 1.0 / np.sqrt(D)
        Wv = jax.random.normal(ks[1], (D, D), dtype=jnp.float32) * s
        bv = jax.random.normal(ks[2], (D,), dtype=jnp.float32) * s
        Wo = jax.random.normal(ks[3], (D, D), dtype=jnp.float32) * s
        bo = jax.random.normal(ks[4], (D,), dtype=jnp.float32) * s
        w = jnp.asarray(DECAY ** np.arange(H), dtype=jnp.float32)
        decay_w = w / jnp.sum(w)
        return {'x': x, 'Wv': Wv, 'bv': bv, 'Wo': Wo, 'bo': bo, 'decay_w': decay_w}
    _L0_tok_all = _L0_tok_setup()
    _L0_tok_in = {k: v for k, v in _L0_tok_all.items() if k in ('Wv', 'bv', 'Wo', 'bo', 'decay_w')}
    del _L0_tok_all

    def _L0_attn_setup():
        import jax, jax.numpy as jnp
        import numpy as np
        import math
        D_MODEL = 256
        N_HEADS = 16
        D_HEAD = D_MODEL // N_HEADS
        WINDOW = 64
        SCALE = 1.0 / math.sqrt(D_HEAD)

        def _window_mask(seq_len: int) -> jnp.ndarray:
            i = jnp.arange(seq_len)[:, None]
            j = jnp.arange(seq_len)[None, :]
            allowed = (j <= i) & (j > i - WINDOW)
            return jnp.where(allowed, 0.0, -jnp.inf).astype(jnp.float32)
        key = jax.random.key(seed)
        kx, kqkv, kout = jax.random.split(key, 3)
        x = jax.random.normal(kx, (2, 512, D_MODEL), dtype=jnp.float32)
        lim_qkv = math.sqrt(6.0 / (D_MODEL + 3 * D_MODEL))
        W_qkv = jax.random.uniform(kqkv, (D_MODEL, 3 * D_MODEL), dtype=jnp.float32, minval=-lim_qkv, maxval=lim_qkv)
        lim_out = math.sqrt(6.0 / (D_MODEL + D_MODEL))
        W_out = jax.random.uniform(kout, (D_MODEL, D_MODEL), dtype=jnp.float32, minval=-lim_out, maxval=lim_out)
        return {'x': x, 'W_qkv': W_qkv, 'W_out': W_out}
    _L0_attn_all = _L0_attn_setup()
    _L0_attn_in = {k: v for k, v in _L0_attn_all.items() if k in ('W_qkv', 'W_out')}
    del _L0_attn_all

    def _L0_ffn_setup():
        import jax, jax.numpy as jnp
        import numpy as np
        TOP_K = 2
        LOGIT_SCALE = 1.0
        key = jax.random.key(seed)
        k = jax.random.split(key, 5)
        B, S, C = (1, 256, 256)
        E, I = (8, 256)
        x = jax.random.normal(k[0], (B, S, C), dtype=jnp.float32)
        router_w = jax.random.normal(k[1], (E, C), dtype=jnp.float32) * 0.02
        w_in = jax.random.normal(k[2], (E, 2 * I, C), dtype=jnp.float32) * 0.02
        b_in = jnp.zeros((E, 2 * I), dtype=jnp.float32)
        w_out = jax.random.normal(k[3], (E, C, I), dtype=jnp.float32) * 0.02
        b_out = jnp.zeros((E, C), dtype=jnp.float32)
        return {'x': x, 'router_w': router_w, 'w_in': w_in, 'b_in': b_in, 'w_out': w_out, 'b_out': b_out}
    _L0_ffn_all = _L0_ffn_setup()
    _L0_ffn_in = {k: v for k, v in _L0_ffn_all.items() if k in ('router_w', 'w_in', 'b_in', 'w_out', 'b_out')}
    del _L0_ffn_all
    return {'x': x, 'L0_tok_Wv': _L0_tok_in['Wv'], 'L0_tok_bv': _L0_tok_in['bv'], 'L0_tok_Wo': _L0_tok_in['Wo'], 'L0_tok_bo': _L0_tok_in['bo'], 'L0_tok_decay_w': _L0_tok_in['decay_w'], 'L0_attn_W_qkv': _L0_attn_in['W_qkv'], 'L0_attn_W_out': _L0_attn_in['W_out'], 'L0_ffn_router_w': _L0_ffn_in['router_w'], 'L0_ffn_w_in': _L0_ffn_in['w_in'], 'L0_ffn_b_in': _L0_ffn_in['b_in'], 'L0_ffn_w_out': _L0_ffn_in['w_out'], 'L0_ffn_b_out': _L0_ffn_in['b_out']}

def reference(x, L0_tok_Wv, L0_tok_bv, L0_tok_Wo, L0_tok_bo, L0_tok_decay_w, L0_attn_W_qkv, L0_attn_W_out, L0_ffn_router_w, L0_ffn_w_in, L0_ffn_b_in, L0_ffn_w_out, L0_ffn_b_out):
    import jax
    import jax.numpy as jnp

    def _L0_tok_ref(x, Wv, bv, Wo, bo, decay_w):
        import jax, jax.numpy as jnp
        import numpy as np
        H = 32
        DECAY = 0.9
        B, T, D = x.shape
        Hlen = decay_w.shape[0]
        x_pad = jnp.pad(x, ((0, 0), (Hlen, 0), (0, 0)))
        kernel = jnp.broadcast_to(decay_w[:, None, None], (Hlen, 1, D))
        s = jax.lax.conv_general_dilated(x_pad, kernel, window_strides=(1,), padding='VALID', dimension_numbers=('NWC', 'WIO', 'NWC'), feature_group_count=D)
        attended = s @ Wv.T + bv * jnp.sum(decay_w)
        return attended @ Wo.T + bo

    def _L0_attn_ref(x, W_qkv, W_out):
        import jax, jax.numpy as jnp
        import numpy as np
        import math
        D_MODEL = 256
        N_HEADS = 16
        D_HEAD = D_MODEL // N_HEADS
        WINDOW = 64
        SCALE = 1.0 / math.sqrt(D_HEAD)

        def _window_mask(seq_len: int) -> jnp.ndarray:
            i = jnp.arange(seq_len)[:, None]
            j = jnp.arange(seq_len)[None, :]
            allowed = (j <= i) & (j > i - WINDOW)
            return jnp.where(allowed, 0.0, -jnp.inf).astype(jnp.float32)
        B, S, _ = x.shape
        qkv = x @ W_qkv
        qkv = qkv.reshape(B, S, 3, N_HEADS, D_HEAD)
        qkv = jnp.transpose(qkv, (2, 0, 3, 1, 4))
        q, k, v = (qkv[0], qkv[1], qkv[2])
        scores = jnp.einsum('bhsd,bhtd->bhst', q, k) * SCALE
        scores = scores + _window_mask(S)[None, None]
        weights = jax.nn.softmax(scores, axis=-1)
        out = jnp.einsum('bhst,bhtd->bhsd', weights, v)
        out = jnp.transpose(out, (0, 2, 1, 3)).reshape(B, S, D_MODEL)
        return out @ W_out

    def _L0_ffn_ref(x, router_w, w_in, b_in, w_out, b_out):
        import jax, jax.numpy as jnp
        import numpy as np
        TOP_K = 2
        LOGIT_SCALE = 1.0
        B, S, C = x.shape
        E = router_w.shape[0]
        xt = x.reshape(-1, C)
        T = xt.shape[0]
        logits = xt @ router_w.T * LOGIT_SCALE
        probs = jax.nn.softmax(logits, axis=-1)
        top_w, top_idx = jax.lax.top_k(probs, TOP_K)
        gate = jnp.zeros((T, E), dtype=probs.dtype)
        gate = gate.at[jnp.arange(T)[:, None], top_idx].set(top_w)
        h = jnp.einsum('tc,eoc->teo', xt, w_in) + b_in
        g, u = jnp.split(h, 2, axis=-1)
        a = jax.nn.silu(g) * u
        y = jnp.einsum('tei,eci->tec', a, w_out) + b_out
        out = jnp.einsum('te,tec->tc', gate, y)
        return out.reshape(B, S, C)
    h = _L0_tok_ref(x, L0_tok_Wv, L0_tok_bv, L0_tok_Wo, L0_tok_bo, L0_tok_decay_w)
    h = h + _L0_attn_ref(_layernorm(h, axis=-1), L0_attn_W_qkv, L0_attn_W_out)
    h = h + _L0_ffn_ref(_layernorm(h, axis=-1), L0_ffn_router_w, L0_ffn_w_in, L0_ffn_b_in, L0_ffn_w_out, L0_ffn_b_out)
    return h

_drawn_inputs = setup_inputs


def setup_inputs(seed=0):
    import zlib

    import numpy as np

    out = dict(_drawn_inputs(seed))
    spreads = {'L0_ffn_b_in': (0.0, 0.8), 'L0_ffn_b_out': (0.0, 0.486)}
    factors = {'L0_ffn_w_in': 6.038, 'L0_ffn_w_out': 5.939}
    for name, (base, spread) in spreads.items():
        noise = np.random.default_rng([zlib.crc32(name.encode()), seed]).standard_normal(out[name].shape)
        drawn = base * np.exp(spread * noise) if base else spread * noise
        out[name] = jnp.asarray(drawn.astype(out[name].dtype))
    for name, factor in factors.items():
        out[name] = (out[name] * factor).astype(out[name].dtype)
    return out
```

```python
from contextlib import ExitStack

import concourse.bass as bass
from concourse import mybir

ALU = mybir.AluOpType
ACT = mybir.ActivationFunctionType
AX = mybir.AxisListType
F32 = mybir.dt.float32
F32R = mybir.dt.float32r
BF16 = mybir.dt.bfloat16

P = 128
B, T, D = 8, 750, 256
TAPS = 32
S = T + 1
NT = -(-S // P)
SP_ = NT * P
DC = D // P
H, HD = 16, 16
HC = H // DC
W = 64
NB = SP_ // W
KP = W + SP_
E, I = 8, 256
BIG = 1e30
EPS = 1e-5
SCALE = float(HD) ** -0.5
DVE_STEPS = 24
BANDW = P + TAPS

ACT_FILLS = 3 + 3 + 3 + 3 + 1 + 2 * NB + 3 + 3
DVE_FILLS = 3 + 3 + NT * H // 2 + NT + 3 + 1
RING = 3


def token_mixer_and_attention(nc, x, wv, bv, wo_t, bo, decay_rev, w_qkv, w_out, router_t,
                              band_dram, h2_dram, xn2t_dram, gates):
    with ExitStack() as ctx:
        def sb(name, shape, dt=F32):
            return ctx.enter_context(nc.sbuf_tensor(name, shape, dt))

        def sem(name):
            return ctx.enter_context(nc.semaphore(name))

        act_bank = ctx.enter_context(nc.psum_tensor("act_bank", [P, RING, 512], F32))
        dve_bank = ctx.enter_context(nc.psum_tensor("dve_bank", [P, RING, 512], F32))
        out_bank = ctx.enter_context(nc.psum_tensor("out_bank", [P, 2, 512], F32))

        ident = sb("ident", [P, P])
        ident_b = sb("ident_b", [P, P], BF16)
        band = sb("band", [P, BANDW])
        key_mask = sb("key_mask", [P, 2, 2, P + W], BF16)
        query_mask = sb("query_mask", [W + 3, 2, P], BF16)
        half_neg = sb("half_neg", [P, NT])
        decay = sb("decay", [P, TAPS])
        wv_sb = sb("wv_sb", [P, DC, D])
        wo_sb = sb("wo_sb", [P, DC, D])
        mix_w = sb("mix_w", [P, DC, D])
        bias_h = sb("bias_h", [P, D])
        bv_sb = sb("bv_sb", [P, DC])
        decay_sum = sb("decay_sum", [P, 1])
        bv_sum = sb("bv_sum", [P, DC])
        bv_wide = sb("bv_wide", [P, DC, P])
        wqkv_sb = sb("wqkv_sb", [P, DC, 3 * D])
        wout_sb = sb("wout_sb", [P, DC, D])
        rt_sb = sb("rt_sb", [P, DC, E])
        expert_no = sb("expert_no", [P, NT, E])

        x_sb = sb("x_sb", [P, NT, D])
        st = sb("st", [P, DC, SP_])
        h = sb("h", [P, NT, D])
        xn = sb("xn", [P, NT, D])
        xnt = sb("xnt", [P, DC, SP_])
        qt = sb("qt", [P, DC, SP_])
        qt_r = sb("qt_r", [P, DC, SP_], F32R)
        kt = sb("kt", [P, DC, KP])
        kt_r = sb("kt_r", [P, DC, KP], F32R)
        q_heads = sb("q_heads", [P, DC, HC, SP_])
        k_heads = sb("k_heads", [P, DC, HC // 2, KP], F32R)
        v_a = sb("v_a", [P, NT, H, 2 * HD])
        v_b = sb("v_b", [P, NT, H, 2 * HD])
        qmask_and_max = sb("qmask_and_max", [W + 3, H, SP_], BF16)
        neg_max = sb("neg_max", [P, NT, H])
        max_rest = sb("max_rest", [P, NT, H])
        max_parts = sb("max_parts", [P, NT, 3, H], BF16)
        max_t = sb("max_t", [3 * H, SP_], BF16)
        probs = kt_r[:, :, :].rearrange("p c k -> p (c k)")[:, 0:3 * HC * W].bitcast(F32).rearrange(
            "p (r h q) -> p r h q", r=3, h=HC)
        out_t = sb("out_t", [P, 2, 4, P])
        recip = sb("recip", [P, 2, H])
        attn = xn[:, :, :].rearrange("p i (h d) -> p i h d", h=H)
        attn_t = xnt[:, :, :]
        h2 = h[:, :, :]
        xn2t = st[:, :, :]
        zeros = x_sb[:, :, :].rearrange("p i d -> p (i d)")[:, 0:161]
        stats = sb("stats", [P, NT, 6])
        moments = sb("moments", [P, NT, 2])
        var_eps = sb("var_eps", [P, NT])
        rstd = sb("rstd", [P, NT])
        logits = sb("logits", [P, NT, E])
        top_logit = sb("top_logit", [P, NT])
        shifted = sb("shifted", [P, NT, E])
        exps = sb("exps", [P, NT, E])
        exp_sum = sb("exp_sum", [P, NT])
        exp_rec = sb("exp_rec", [P, NT])
        rprobs = sb("rprobs", [P, NT, E])
        best = sb("best", [P, NT, 8])
        best_at = sb("best_at", [P, NT, 8], mybir.dt.uint32)
        best_at_f = sb("best_at_f", [P, NT, 8])
        hot0 = sb("hot0", [P, NT, E])
        hot1 = sb("hot1", [P, NT, E])
        chosen = sb("chosen", [P, NT, E])

        weights_in = sem("weights_in")
        small_in = sem("small_in")
        band_zeroed = sem("band_zeroed")
        band_written = sem("band_written")
        band_in = sem("band_in")
        consts_ready = sem("consts_ready")
        zeros_ready = sem("zeros_ready")
        pool_chain = sem("pool_chain")
        dve_passed = sem("dve_passed")
        pe_passed = sem("pe_passed")
        pool_passed = sem("pool_passed")
        setup_chain = sem("setup_chain")
        setup_mm = sem("setup_mm")
        mix_ready = sem("mix_ready")
        x_in = sem("x_in")
        conv_done = sem("conv_done")
        act_filled = sem("act_filled")
        act_copied = sem("act_copied")
        dve_filled = sem("dve_filled")
        dve_copied = sem("dve_copied")
        out_copied = sem("out_copied")
        xn_ready = sem("xn_ready")
        dve_chain = sem("dve_chain")
        var_ready = sem("var_ready")
        rstd_ready = sem("rstd_ready")
        q_rounded = sem("q_rounded")
        k_rounded = sem("k_rounded")
        q_placed = sem("q_placed")
        k_placed = sem("k_placed")
        v_shifted = sem("v_shifted")
        parts_ready = sem("parts_ready")
        max_placed = sem("max_placed")
        maxes_done = sem("maxes_done")
        probs_used = sem("probs_used")
        attn_ready = sem("attn_ready")
        h2_saved = sem("h2_saved")
        xn2t_saved = sem("xn2t_saved")
        shifted_ready = sem("shifted_ready")
        exps_ready = sem("exps_ready")

        def act_free(b, k):
            return b * ACT_FILLS + max(k + 1, RING)

        def act_has(b, k):
            return b * ACT_FILLS + k + 1 + RING

        def dve_free(b, k):
            return b * DVE_FILLS + max(k + 1, RING)

        def dve_has(b, k):
            return b * DVE_FILLS + k + 1 + RING

        def probs_before(b):
            return b * 2 * NB + 3

        A_ST, A_XNT, A_Q, A_V = 0, 3, 6, 9
        A_MAX, A_SC = 12, 13
        A_AT, A_X2 = A_SC + 2 * NB, A_SC + 2 * NB + 3
        D_H, D_K, D_MAX = 0, 3, 6
        D_OUT = D_MAX + NT * H // 2
        D_PROJ, D_ROUTE = D_OUT + NT, D_OUT + NT + 3
        assert A_X2 + 3 == ACT_FILLS and D_ROUTE + 1 == DVE_FILLS
        N_PLACE = DC * HC * 16

        def thirds(dst, bank, off=0):
            return [(dst[:, 0, off:off + 512], bank[:, 0:512]),
                    (dst[:, 1, off:off + 512], bank[:, 0:512]),
                    (dst[:, 0:2, off + 512:off + SP_], bank[:, 0:512].rearrange("p (c n) -> p c n", c=2))]

        block = ctx.enter_context(nc.Block())

        @block.sync
        def _(sp):
            sp.dma_start(wv_sb[:, :, :], wv.rearrange("(c p) n -> p c n", p=P)).then_inc(weights_in, 16)
            sp.dma_start(wo_sb[:, :, :], wo_t.rearrange("(c p) n -> p c n", p=P)).then_inc(weights_in, 16)
            sp.dma_start(wqkv_sb[:, :, :], w_qkv.rearrange("(c p) n -> p c n", p=P)).then_inc(weights_in, 16)
            sp.dma_start(wout_sb[:, :, :], w_out.rearrange("(c p) n -> p c n", p=P)).then_inc(weights_in, 16)
            sp.dma_start(rt_sb[:, :, :], router_t.rearrange("(c p) n -> p c n", p=P)).then_inc(weights_in, 16)
            sp.wait_ge(zeros_ready, 1)
            sp.dma_start(band_dram[0:P * 161].rearrange("(p j) -> p j", j=161), zeros).then_inc(band_zeroed, 16)
            sp.wait_ge(band_zeroed, 16)
            sp.wait_ge(small_in, 48)
            sp.dma_start(band_dram[1:1 + P * 161].rearrange("(p j) -> p j", j=161)[:, 0:TAPS],
                         decay[:, :]).then_inc(band_written, 16)
            sp.wait_ge(band_written, 16)
            sp.dma_start(band[:, :], band_dram[0:P * BANDW].rearrange("(p j) -> p j", j=BANDW)).then_inc(band_in, 16)
            sp.wait_ge(consts_ready, 14)
            with sp.Fori(0, B) as b:
                sp.wait_ge(act_copied, act_has(b, A_Q + 2))
                sp.wait_ge(probs_used, probs_before(b))
                for c in range(DC):
                    for g in range(HC):
                        sp.dma_start(q_heads[g * HD:(g + 1) * HD, c, g, :],
                                     qt[g * HD:(g + 1) * HD, c, :]).then_inc(q_placed, 16)
                sp.wait_ge(k_rounded, b + 1)
                sp.wait_ge(maxes_done, b)
                for c in range(DC):
                    for g in range(HC):
                        sp.dma_start(k_heads[g * HD:(g + 1) * HD, c, g % (HC // 2), :].bitcast(F32),
                                     kt_r[g * HD:(g + 1) * HD, c, :].bitcast(F32)).then_inc(k_placed, 16)
                sp.wait_ge(act_copied, act_has(b, A_V + 2))
                sp.wait_ge(probs_used, probs_before(b))
                sp.dma_start(v_b[W:P, :, :, :], v_a[0:W, :, :, :]).then_inc(v_shifted, 16)
                sp.dma_start(v_b[0:W, 1:NT, :, :], v_a[W:P, 0:NT - 1, :, :]).then_inc(v_shifted, 16)
                sp.wait_ge(act_copied, act_has(b, A_MAX))
                for k in range(3):
                    sp.dma_start(qmask_and_max[W + k:W + k + 1, :, :],
                                 max_t[k * H:(k + 1) * H, :]).then_inc(max_placed, 16)
                sp.wait_ge(dve_copied, dve_has(b, D_PROJ + 2))
                sp.dma_start(h2_dram[b, :, :, :], h2[:, :, :]).then_inc(h2_saved, 16)
                sp.wait_ge(act_copied, act_has(b, A_X2 + 2))
                sp.dma_start(xn2t_dram[b, :, :, :], xn2t[:, :, :]).then_inc(xn2t_saved, 16)
            sp.wait_ge(h2_saved, B * 16)
            sp.wait_ge(xn2t_saved, B * 16)

        @block.gpsimd
        def _(pool):
            pool.memset(zeros, 0.0).then_inc(zeros_ready, 1)
            pool.dma_start(decay[:, :], decay_rev.partition_broadcast(P)).then_inc(small_in, 16)
            pool.dma_start(bv_sb[:, :], bv).then_inc(small_in, 16)
            pool.dma_start(bias_h[:, :], bo.partition_broadcast(P)).then_inc(small_in, 16)
            pool.memset(ident[:, :], 1.0).then_inc(pool_chain, 1)
            pool.memset(ident_b[:, :], 1.0).then_inc(pool_chain, 1)
            pool.memset(qmask_and_max[0:W, :, :], 1.0).then_inc(pool_chain, 1)
            pool.memset(query_mask[0:W, :, :], 0.0).then_inc(pool_chain, 1)
            pool.memset(key_mask[:, :, :, :], 0.0).then_inc(pool_chain, 1)
            pool.wait_ge(pool_chain, 5)
            pool.affine_select(ident[:, :], ident[:, :], [[-1, P]], ALU.is_equal, 0.0, base=0,
                               channel_multiplier=1).then_inc(consts_ready, 1)
            pool.affine_select(ident_b[:, :], ident_b[:, :], [[-1, P]], ALU.is_equal, 0.0, base=0,
                               channel_multiplier=1).then_inc(consts_ready, 1)
            im = qmask_and_max[0:W, :, :].rearrange("p h (n w) -> p (h n) w", w=W)
            pool.affine_select(im, im, [[0, H * NB], [-1, W]], ALU.is_equal, 0.0, base=0,
                               channel_multiplier=1).then_inc(consts_ready, 1)
            qm = query_mask[0:W, :, :]
            pool.affine_select(qm, qm, [[0, 2], [1, P]], ALU.is_gt, -BIG, base=0,
                               channel_multiplier=-1).then_inc(pool_chain, 1)
            pool.wait_ge(pool_chain, 6)
            pool.affine_select(qm, qm, [[0, 2], [-1, P]], ALU.is_ge, -BIG, base=W,
                               channel_multiplier=1).then_inc(pool_chain, 1)
            pool.wait_ge(pool_chain, 7)
            qm0 = query_mask[0:W, 0, :]
            pool.affine_select(qm0, qm0, [[1, P]], ALU.is_ge, -BIG, base=-W,
                               channel_multiplier=0).then_inc(consts_ready, 1)
            km = key_mask[:, :, :, :].rearrange("p a b k -> p (a b) k")
            pool.affine_select(km, km, [[0, 4], [1, P + W]], ALU.is_gt, -BIG, base=0,
                               channel_multiplier=-1).then_inc(pool_chain, 1)
            pool.wait_ge(pool_chain, 8)
            pool.affine_select(km, km, [[0, 4], [-1, P + W]], ALU.is_ge, -BIG, base=W,
                               channel_multiplier=1).then_inc(pool_chain, 1)
            pool.wait_ge(pool_chain, 9)
            km0 = key_mask[:, 0, :, :]
            pool.affine_select(km0, km0, [[0, 2], [1, P + W]], ALU.is_ge, -BIG, base=-W,
                               channel_multiplier=0).then_inc(consts_ready, 1)
            pool.memset(half_neg[:, :], -0.5).then_inc(consts_ready, 1)
            pool.memset(q_heads[:, :, :, :], 0.0).then_inc(consts_ready, 1)
            pool.memset(k_heads[:, :, :, :].bitcast(F32), 0.0).then_inc(consts_ready, 1)
            pool.iota(expert_no[:, :, :], [[0, NT], [1, E]], base=0, channel_multiplier=0,
                      allow_small_or_imprecise_dtypes=True).then_inc(consts_ready, 1)
            pool.wait_ge(consts_ready, 14)
            pool.wait_ge(band_zeroed, 16)
            with pool.Fori(0, B) as b:
                pool.wait_ge(conv_done, b)
                pool.dma_start(x_sb[:, 0:NT - 1, :],
                               x[b, 0:(NT - 1) * P, :].rearrange("(i p) d -> p i d", p=P)).then_inc(x_in, 16)
                pool.dma_start(x_sb[0:T - (NT - 1) * P, NT - 1, :], x[b, (NT - 1) * P:T, :]).then_inc(x_in, 16)
                pool.wait_ge(var_ready, 2 * b + 1)
                pool.tensor_tensor(rstd[:, :], var_eps[:, :], half_neg[:, :], ALU.pow).then_inc(rstd_ready, 1)
                pool.wait_ge(act_copied, act_has(b, A_Q + 2))
                pool.sem_inc(pool_passed, 1)
                pool.tensor_copy(qt_r[:, :, :], qt[:, :, :]).then_inc(q_rounded, 1)
                pool.wait_ge(dve_copied, dve_has(b, D_K + 2))
                pool.wait_ge(k_placed, b * N_PLACE)
                pool.sem_inc(pool_passed, 1)
                pool.tensor_copy(kt_r[:, :, :], kt[:, :, :]).then_inc(k_rounded, 1)
                pool.wait_ge(var_ready, 2 * b + 2)
                pool.tensor_tensor(rstd[:, :], var_eps[:, :], half_neg[:, :], ALU.pow).then_inc(rstd_ready, 1)

        @block.scalar
        def _(act):
            act.wait_ge(setup_mm, 1)
            act.copy(mix_w[:, :, :], act_bank[:, 0, :].rearrange("p (c n) -> p c n", c=DC)).then_inc(mix_ready, 1)
            act.wait_ge(mix_ready, 1)
            act.sem_inc(act_copied, RING)
            with act.Fori(0, B) as b:
                def bank(k):
                    return act_bank[:, (A0 + k) % RING, :]
                A0 = 0

                def fill(k):
                    act.wait_ge(act_filled, b * ACT_FILLS + k + 1)

                act.wait_ge(xn2t_saved, b * 16)
                for k in range(3):
                    fill(A_ST + k)
                    d, s = thirds(st, bank(A_ST + k))[k]
                    act.copy(d, s).then_inc(act_copied, 1)
                for k in range(3):
                    fill(A_XNT + k)
                    d, s = thirds(xnt, bank(A_XNT + k))[k]
                    act.copy(d, s).then_inc(act_copied, 1)
                act.wait_ge(q_placed, b * N_PLACE)
                act.wait_ge(q_rounded, b)
                for k in range(3):
                    fill(A_Q + k)
                    d, s = thirds(qt, bank(A_Q + k))[k]
                    act.mul(d, s, SCALE).then_inc(act_copied, 1)
                act.wait_ge(v_shifted, b * 32)
                for k in range(3):
                    fill(A_V + k)
                    act.copy(v_a[:, 2 * k:2 * k + 2, :, 0:HD],
                             bank(A_V + k).rearrange("p (i h d) -> p i h d", i=2, h=H)).then_inc(act_copied, 1)
                fill(A_MAX)
                act.wait_ge(max_placed, b * 48)
                act.copy(max_t[:, :], bank(A_MAX).bitcast(BF16)[0:3 * H, 0:SP_]).then_inc(act_copied, 1)
                for n in range(2 * NB):
                    fill(A_SC + n)
                    act.wait_ge(probs_used, b * 2 * NB + n + 1)
                    act.activation(probs[:, n % 3, :, :], bank(A_SC + n).rearrange("p (h q) -> p h q", h=HC),
                                   ACT.Exp).then_inc(act_copied, 1)
                for k in range(3):
                    fill(A_AT + k)
                    d, s = thirds(attn_t, bank(A_AT + k))[k]
                    act.copy(d, s).then_inc(act_copied, 1)
                for k in range(3):
                    fill(A_X2 + k)
                    d, s = thirds(xn2t, bank(A_X2 + k))[k]
                    act.copy(d, s).then_inc(act_copied, 1)
                act.wait_ge(shifted_ready, b + 1)
                act.activation(exps[:, :, :], shifted[:, :, :], ACT.Exp).then_inc(exps_ready, 1)

        @block.vector
        def _(dve):
            chain = [0]

            def step(ins, base, n):
                chain[0] += 1
                ins.then_inc(dve_chain, 1)
                dve.wait_ge(dve_chain, base + chain[0])

            dve.memset(query_mask[W:W + 3, :, :], 1.0).then_inc(consts_ready, 1)
            dve.memset(x_sb[96:P, NT - 1, :], 0.0).then_inc(consts_ready, 1)
            dve.memset(v_a[:, :, :, HD:2 * HD], 1.0).then_inc(consts_ready, 1)
            dve.memset(v_b[0:W, 0, :, :], 0.0).then_inc(consts_ready, 1)
            dve.memset(kt[:, :, 0:W], 0.0).then_inc(consts_ready, 1)
            dve.wait_ge(small_in, 48)
            dve.tensor_reduce(decay_sum[:, :], decay[:, :], AX.X, ALU.add).then_inc(setup_chain, 1)
            dve.wait_ge(setup_chain, 1)
            dve.tensor_scalar(bv_sum[:, :], bv_sb[:, :], decay_sum[:, 0:1], None, ALU.mult).then_inc(setup_chain, 1)
            dve.wait_ge(setup_chain, 2)
            dve.tensor_copy(bv_wide[:, :, :], bv_sum[:, :].unsqueeze(2).to_broadcast([P, DC, P])).then_inc(setup_chain, 1)
            dve.wait_ge(setup_mm, 2)
            dve.tensor_tensor(bias_h[:, :], dve_bank[:, 0, 0:D], bias_h[:, :], ALU.add).then_inc(dve_copied, RING)
            dve.sem_inc(out_copied, 2)
            dve.wait_ge(dve_copied, RING)
            dve.wait_ge(consts_ready, 14)
            with dve.Fori(0, B) as b:
                base = b * DVE_STEPS
                chain[0] = 0

                def st_(ins):
                    step(ins, base, 0)

                def bank(k):
                    return dve_bank[:, k % RING, :]

                def fill(k):
                    dve.wait_ge(dve_filled, b * DVE_FILLS + k + 1)

                def layer_norm(src, pass_no):
                    for i in range(NT):
                        last = dve.bn_stats(stats[:, i, :], src[:, i, :])
                    st_(last)
                    dve.sem_inc(dve_passed, 1)
                    for i in range(NT):
                        last = dve.bn_aggr(moments[:, i, :], stats[:, i, :])
                    st_(last)
                    dve.tensor_scalar(var_eps[:, :], moments[:, :, 1], EPS, None, ALU.add).then_inc(var_ready, 1)
                    dve.wait_ge(rstd_ready, 2 * b + 1 + pass_no)
                    for i in range(NT):
                        dve.tensor_scalar(xn[:, i, :], src[:, i, :], moments[:, i, 0:1], rstd[:, i:i + 1],
                                          ALU.subtract, ALU.mult).then_inc(xn_ready, 1)

                dve.wait_ge(h2_saved, b * 16)
                for k in range(3):
                    fill(D_H + k)
                    last = dve.tensor_tensor(h[:, 2 * k:2 * k + 2, :],
                                             bank(D_H + k).rearrange("p (i d) -> p i d", i=2),
                                             bias_h[:, :].unsqueeze(1).to_broadcast([P, 2, D]), ALU.add)
                    last.then_inc(dve_copied, 1)
                dve.wait_ge(dve_copied, dve_has(b, D_H + 2))
                layer_norm(h, 0)
                dve.wait_ge(k_rounded, b)
                for k in range(3):
                    fill(D_K + k)
                    d, s = thirds(kt, bank(D_K + k), W)[k]
                    dve.tensor_copy(d, s).then_inc(dve_copied, 1)
                for n in range(NT * H // 2):
                    i, g = divmod(n, H // 2)
                    fill(D_MAX + n)
                    dve.tensor_reduce(neg_max[:, i, 2 * g:2 * g + 2],
                                      bank(D_MAX + n)[:, 0:2 * (P + W)].rearrange("p (h k) -> p h k", h=2),
                                      AX.X, ALU.max, negate=True).then_inc(dve_copied, 1)
                dve.wait_ge(dve_copied, dve_has(b, D_OUT - 1))
                st_(dve.tensor_copy(max_parts[:, :, 0, :], neg_max[:, :, :]))
                st_(dve.tensor_tensor(max_rest[:, :, :], neg_max[:, :, :], max_parts[:, :, 0, :], ALU.subtract))
                st_(dve.tensor_copy(max_parts[:, :, 1, :], max_rest[:, :, :]))
                st_(dve.tensor_tensor(max_rest[:, :, :], max_rest[:, :, :], max_parts[:, :, 1, :], ALU.subtract))
                dve.tensor_copy(max_parts[:, :, 2, :], max_rest[:, :, :]).then_inc(parts_ready, 1)
                for i in range(NT + 1):
                    if i < NT:
                        dve.wait_ge(probs_used, probs_before(b) + 4 * (i + 1))
                        dve.tensor_copy(out_t[:, i % 2, :, :],
                                        out_bank[:, i % 2, :].rearrange("p (g q) -> p g q", g=4)).then_inc(out_copied, 1)
                    if i >= 1:
                        j = i - 1
                        fill(D_OUT + j)
                        back = bank(D_OUT + j).rearrange("p (h d) -> p h d", d=2 * HD)
                        st_(dve.reciprocal(recip[:, j % 2, :], back[:, :, HD]))
                        dve.tensor_tensor(attn[:, j, :, :], back[:, :, 0:HD],
                                          recip[:, j % 2, :].unsqueeze(2).to_broadcast([P, H, HD]),
                                          ALU.mult).then_inc(dve_copied, 1)
                for k in range(3):
                    fill(D_PROJ + k)
                    dve.tensor_tensor(h2[:, 2 * k:2 * k + 2, :],
                                      bank(D_PROJ + k).rearrange("p (i d) -> p i d", i=2),
                                      h[:, 2 * k:2 * k + 2, :], ALU.add).then_inc(dve_copied, 1)
                dve.wait_ge(dve_copied, dve_has(b, D_PROJ + 2))
                layer_norm(h2, 1)
                fill(D_ROUTE)
                dve.tensor_copy(logits[:, :, :],
                                bank(D_ROUTE)[:, 0:NT * E].rearrange("p (i e) -> p i e", e=E)).then_inc(dve_copied, 1)
                dve.wait_ge(dve_copied, dve_has(b, D_ROUTE))
                st_(dve.tensor_reduce(top_logit[:, :], logits[:, :, :], AX.X, ALU.max))
                dve.tensor_tensor(shifted[:, :, :], logits[:, :, :],
                                  top_logit[:, :].unsqueeze(2).to_broadcast([P, NT, E]),
                                  ALU.subtract).then_inc(shifted_ready, 1)
                dve.wait_ge(exps_ready, b + 1)
                st_(dve.tensor_reduce(exp_sum[:, :], exps[:, :, :], AX.X, ALU.add))
                st_(dve.reciprocal(exp_rec[:, :], exp_sum[:, :]))
                st_(dve.tensor_tensor(rprobs[:, :, :], exps[:, :, :],
                                      exp_rec[:, :].unsqueeze(2).to_broadcast([P, NT, E]), ALU.mult))
                dve.sem_inc(dve_passed, 1)
                for i in range(NT):
                    last = dve.max(best[:, i, :], rprobs[:, i, :])
                st_(last)
                dve.sem_inc(dve_passed, 1)
                for i in range(NT):
                    last = dve.max_index(best_at[:, i, :], best[:, i, :], rprobs[:, i, :])
                st_(last)
                st_(dve.tensor_copy(best_at_f[:, :, :], best_at[:, :, :]))
                dve.tensor_tensor(hot0[:, :, :], expert_no[:, :, :],
                                  best_at_f[:, :, 0:1].to_broadcast([P, NT, E]), ALU.is_equal)
                st_(dve.tensor_tensor(hot1[:, :, :], expert_no[:, :, :],
                                      best_at_f[:, :, 1:2].to_broadcast([P, NT, E]), ALU.is_equal))
                st_(dve.tensor_tensor(chosen[:, :, :], hot0[:, :, :], hot1[:, :, :], ALU.add))
                st_(dve.tensor_tensor(gates[:, bass.ts(b, NT), :], chosen[:, :, :], rprobs[:, :, :], ALU.mult))
                assert chain[0] == DVE_STEPS, chain[0]

        @block.tensor
        def _(pe):
            pe.wait_ge(weights_in, 80)
            pe.wait_ge(setup_chain, 3)
            for m in range(DC):
                for c in range(DC):
                    last = pe.matmul(act_bank[:, 0, m * D:(m + 1) * D], wv_sb[:, c, m * P:(m + 1) * P],
                                     wo_sb[:, c, :], start=(c == 0), stop=(c == DC - 1))
            last.then_inc(setup_mm, 1)
            for c in range(DC):
                last = pe.matmul(dve_bank[:, 0, 0:D], bv_wide[:, c, :], wo_sb[:, c, :],
                                 start=(c == 0), stop=(c == DC - 1))
            last.then_inc(setup_mm, 1)
            pe.sem_inc(probs_used, 3)
            pe.wait_ge(band_in, 16)
            pe.wait_ge(consts_ready, 14)
            with pe.Fori(0, B) as b:
                def act_open(k):
                    pe.wait_ge(act_copied, act_free(b, k))
                    return act_bank[:, k % RING, :]

                def dve_open(k):
                    pe.wait_ge(dve_copied, dve_free(b, k))
                    return dve_bank[:, k % RING, :]

                def product(out, stationary, moving):
                    for c in range(DC):
                        last = pe.matmul(out, stationary(c), moving(c), start=(c == 0), stop=(c == DC - 1))
                    return last

                def project(open_, filled, k0, weight, src):
                    for k in range(3):
                        bk = open_(k0 + k)
                        if k < 2:
                            last = product(bk[:, 0:512], lambda c: weight(c, k), lambda c: src[:, c, 0:512])
                        else:
                            for m in range(2):
                                last = product(bk[:, m * 256:(m + 1) * 256], lambda c: weight(c, m),
                                               lambda c: src[:, c, 512:SP_])
                        last.then_inc(filled, 1)

                def turn(k0, src, ready=None):
                    got = 0
                    for k in range(3):
                        bk = act_open(k0 + k)
                        for j in range(4):
                            c, i = (k, j) if k < 2 else (j // 2, 4 + j % 2)
                            if ready is not None and i + 1 > got:
                                got = i + 1
                                ready(got)
                            last = pe.transpose(bk[:, j * P:(j + 1) * P], src[:, i, c * P:(c + 1) * P], ident[:, :])
                        last.then_inc(act_filled, 1)

                pe.wait_ge(x_in, b * 32 + 32)
                for c in range(DC):
                    bk = act_open(A_ST + c)
                    for i in range(4):
                        n = min(BANDW, 512 - i * P)
                        last = pe.matmul(bk[:, i * P:i * P + n], x_sb[:, i, c * P:(c + 1) * P], band[:, 0:n],
                                         start=(i == 0), stop=(i == 3), skip_group_check=True)
                    last.then_inc(act_filled, 1)
                bk = act_open(A_ST + 2)
                for c in range(DC):
                    o = c * 256
                    pe.matmul(bk[:, o:o + TAPS], x_sb[:, 3, c * P:(c + 1) * P], band[:, P:BANDW],
                              start=True, stop=False, skip_group_check=True)
                    for i in range(4, 6):
                        n = min(BANDW, SP_ - i * P)
                        a = o + (i - 4) * P
                        last = pe.matmul(bk[:, a:a + n], x_sb[:, i, c * P:(c + 1) * P], band[:, 0:n],
                                         start=False, stop=(i == 5), skip_group_check=True)
                last.then_inc(act_filled, 1)
                for k in range(3):
                    bk = dve_open(D_H + k)
                    if k == 0:
                        pe.wait_ge(mix_ready, 1)
                        pe.wait_ge(act_copied, act_has(b, A_ST + 1))
                    if k == 2:
                        pe.wait_ge(act_copied, act_has(b, A_ST + 2))
                    for j in range(2):
                        i = 2 * k + j
                        for c in range(DC):
                            last = pe.matmul(bk[:, j * D:(j + 1) * D], st[:, c, i * P:(i + 1) * P], mix_w[:, c, :],
                                             start=(c == 0), stop=(c == DC - 1))
                            if (i, c) == (0, 0):
                                last.then_inc(conv_done, 1)
                    last.then_inc(dve_filled, 1)
                turn(A_XNT, xn, lambda n: pe.wait_ge(xn_ready, 2 * b * NT + n))
                pe.wait_ge(act_copied, act_has(b, A_XNT + 2))
                project(act_open, act_filled, A_Q, lambda c, m: wqkv_sb[:, c, m * P:(m + 1) * P], xnt)
                project(dve_open, dve_filled, D_K, lambda c, m: wqkv_sb[:, c, D + m * P:D + (m + 1) * P], xnt)
                for k in range(3):
                    bk = act_open(A_V + k)
                    for j in range(2):
                        i = 2 * k + j
                        last = product(bk[:, j * D:(j + 1) * D], lambda c: xnt[:, c, i * P:(i + 1) * P],
                                       lambda c: wqkv_sb[:, c, 2 * D:3 * D])
                    last.then_inc(act_filled, 1)
                pe.wait_ge(q_rounded, b + 1)
                pe.wait_ge(k_placed, (b + 1) * N_PLACE)
                for i in range(NT):
                    for g in range(H // 2):
                        n = i * H // 2 + g
                        c, a = divmod(2 * g, HC)
                        bk = dve_open(D_MAX + n)[:, 0:2 * (P + W)]
                        pe.matmul(bk, ident_b[:, :], key_mask[:, min(i, 1), :, :].rearrange("p h k -> p (h k)"),
                                  start=True, stop=False)
                        half, a = divmod(a, HC // 2)
                        rows = slice(half * W, (half + 1) * W)
                        last = pe.matmul(bk.rearrange("p (h k) -> p h k", h=2), qt_r[rows, c, i * P:(i + 1) * P],
                                         k_heads[rows, c, a:a + 2, i * P:i * P + P + W], start=False, stop=True)
                        last.then_inc(dve_filled, 1)
                pe.wait_ge(parts_ready, b + 1)
                bk = act_open(A_MAX).bitcast(BF16)
                pe.sem_inc(pe_passed, 1)
                for i in range(NT):
                    last = pe.transpose(bk[0:3 * H, i * P:(i + 1) * P],
                                        max_parts[:, i, :, :].rearrange("p a h -> p (a h)"), ident_b[:, :])
                    if i == 0:
                        last.then_inc(maxes_done, 1)
                last.then_inc(act_filled, 1)
                pe.wait_ge(max_placed, (b + 1) * 48)
                pe.wait_ge(q_placed, (b + 1) * N_PLACE)

                def scores(n, c):
                    bk = act_open(A_SC + 2 * n + c).rearrange("p (h q) -> p h q", h=HC)
                    pe.matmul(bk, query_mask[:, min(n, 1), :],
                              qmask_and_max[:, c * HC:(c + 1) * HC, n * W:(n + 1) * W], start=True, stop=False)
                    pe.matmul(bk, kt[:, c, n * W:n * W + P], q_heads[:, c, :, n * W:(n + 1) * W],
                              start=False, stop=True).then_inc(act_filled, 1)

                def values(n, c):
                    pe.wait_ge(act_copied, act_has(b, A_SC + 2 * n + c))
                    if n % 2 == 0 and c == 0:
                        pe.wait_ge(out_copied, b * NT + n // 2 + 1)
                    v = v_b[:, n // 2, :, :] if n % 2 == 0 else v_a[:, n // 2, :, :]
                    for a in range(HC):
                        g, r = divmod(c * HC + a, 4)
                        q0 = g * P + (n % 2) * W
                        last = pe.matmul(out_bank[32 * r:32 * r + 32, (n // 2) % 2, q0:q0 + W],
                                         v[:, c * HC + a, :], probs[:, (2 * n + c) % 3, a, :],
                                         start=True, stop=True)
                    return last

                def out_back(i):
                    pe.wait_ge(out_copied, b * NT + i + 1 + 2)
                    bk = dve_open(D_OUT + i)
                    for g in range(4):
                        last = pe.transpose(bk[:, g * P:(g + 1) * P], out_t[:, i % 2, g, :], ident[:, :])
                    last.then_inc(dve_filled, 1)

                pe.wait_ge(v_shifted, (b + 1) * 32)
                for m in range(2 * NB + 2):
                    if m < 2 * NB:
                        scores(*divmod(m, 2))
                    if m >= 2:
                        n, c = divmod(m - 2, 2)
                        last = values(n, c)
                        last.then_inc(probs_used, 1)
                        if n % 2 == 1 and c == 0 and n >= 3:
                            out_back(n // 2 - 1)
                out_back(NT - 1)
                pe.wait_ge(dve_copied, dve_has(b, D_OUT + NT - 1))
                turn(A_AT, attn[:, :, :, :].rearrange("p i h d -> p i (h d)"))
                for k in range(3):
                    bk = dve_open(D_PROJ + k)
                    pe.wait_ge(act_copied, act_has(b, A_AT + 1 if k < 2 else A_AT + 2))
                    for j in range(2):
                        i = 2 * k + j
                        last = product(bk[:, j * D:(j + 1) * D], lambda c: attn_t[:, c, i * P:(i + 1) * P],
                                       lambda c: wout_sb[:, c, :])
                    last.then_inc(dve_filled, 1)
                turn(A_X2, xn, lambda n: pe.wait_ge(xn_ready, (2 * b + 1) * NT + n))
                pe.wait_ge(act_copied, act_has(b, A_X2 + 2))
                bk = dve_open(D_ROUTE)
                for i in range(NT):
                    last = product(bk[:, i * E:(i + 1) * E], lambda c: xn2t[:, c, i * P:(i + 1) * P],
                                   lambda c: rt_sb[:, c, :])
                last.then_inc(dve_filled, 1)


def experts(nc, w_in_t, b_in, w_out_t, b_out, h2_dram, xn2t_dram, gates, out):
    with ExitStack() as ctx:
        def sb(name, shape, dt=F32):
            return ctx.enter_context(nc.sbuf_tensor(name, shape, dt))

        def sem(name):
            return ctx.enter_context(nc.semaphore(name))

        in_bank = ctx.enter_context(nc.psum_tensor("in_bank", [P, 2, 512], F32))
        turn_bank = ctx.enter_context(nc.psum_tensor("turn_bank", [P, 2, 512], F32))
        y_bank = ctx.enter_context(nc.psum_tensor("y_bank", [P, 2, 512], F32))
        gate_bank = ctx.enter_context(nc.psum_tensor("gate_bank", [P, 2, 512], F32))

        ident = sb("ident2", [P, P])
        w_in_sb = sb("w_in_sb", [P, DC, E, 2 * I])
        w_out_sb = sb("w_out_sb", [P, DC, E, D])
        b_in_sb = sb("b_in_sb", [P, E, 2 * I])
        b_out_sb = sb("b_out_sb", [E, D])
        xt = sb("xt", [P, DC, SP_])
        h2 = sb("h2b", [P, NT, D])
        hid = sb("hid", [P, 2, 2 * I])
        act_g = sb("act_g", [P, 2, I])
        prod = sb("prod", [P, 2, I])
        prod_t = sb("prod_t", [P, 2, DC, P])
        gates_now = sb("gates_now", [P, NT, E])
        gates_t = sb("gates_t", [E, 2, P])
        res = sb("res", [P, 2, D])

        w_loaded = sem("w_loaded")
        ident_ready = sem("ident_ready")
        ones_ready = sem("ones_ready")
        xt_in = sem("xt_in")
        h2_in = sem("h2_in")
        hid_filled = sem("hid_filled")
        hid_ready = sem("hid_ready")
        gated = sem("gated")
        prod_ready = sem("prod_ready")
        turned = sem("turned")
        prod_t_ready = sem("prod_t_ready")
        summed = sem("summed")
        gates_turned = sem("gates_turned")
        gates_copied = sem("gates_copied")
        gates_t_ready = sem("gates_t_ready")
        res_ready = sem("res_ready")
        saved = [sem("saved_0"), sem("saved_1")]
        NU = NT * E

        block = ctx.enter_context(nc.Block())

        @block.sync
        def _(sp):
            sp.dma_start(w_in_sb[:, :, :, :], w_in_t.rearrange("(c p) e n -> p c e n", p=P)).then_inc(w_loaded, 16)
            sp.dma_start(w_out_sb[:, :, :, :], w_out_t.rearrange("(c p) e n -> p c e n", p=P)).then_inc(w_loaded, 16)
            sp.dma_start(b_in_sb[:, :, :], b_in.rearrange("e n -> (e n)").partition_broadcast(P)).then_inc(w_loaded, 16)
            sp.dma_start(b_out_sb[:, :], b_out).then_inc(w_loaded, 16)
            with sp.Fori(0, B) as b:
                sp.wait_ge(summed, b * NT)
                sp.dma_start(xt[:, :, :], xn2t_dram[b, :, :, :]).then_inc(xt_in, 16)
                sp.wait_ge(res_ready, b * NT)
                sp.dma_start(h2[:, :, :], h2_dram[b, :, :, :]).then_inc(h2_in, 16)
                for i in range(NT):
                    n = min(P, S - i * P)
                    sp.wait_ge(res_ready, b * NT + i + 1)
                    sp.dma_start(out[b, i * P:i * P + n, :], res[0:n, i % 2, :]).then_inc(saved[i % 2], 16)
            for one in saved:
                sp.wait_ge(one, B * NT // 2 * 16)

        @block.gpsimd
        def _(pool):
            pool.memset(ident[:, :], 1.0).then_inc(ones_ready, 1)
            pool.wait_ge(ones_ready, 1)
            pool.affine_select(ident[:, :], ident[:, :], [[-1, P]], ALU.is_equal, 0.0, base=0,
                               channel_multiplier=1).then_inc(ident_ready, 1)

        @block.scalar
        def _(act):
            with act.Fori(0, B) as b:
                for u in range(NU + 1):
                    if u < NU:
                        act.wait_ge(hid_ready, b * NU + u + 1)
                        act.activation(act_g[:, u % 2, :], hid[:, u % 2, 0:I], ACT.Silu).then_inc(gated, 1)
                    if u >= 1:
                        act.wait_ge(turned, b * NU + u)
                        act.copy(prod_t[:, (u - 1) % 2, :, :],
                                 turn_bank[:, (u - 1) % 2, 0:256].rearrange("p (c n) -> p c n", c=2)).then_inc(prod_t_ready, 1)

        @block.vector
        def _(dve):
            dve.wait_ge(w_loaded, 64)
            with dve.Fori(0, B) as b:
                dve.tensor_copy(gates_now[:, :, :], gates[:, bass.ts(b, NT), :]).then_inc(gates_copied, 1)
                dve.wait_ge(gates_copied, b + 1)
                for u in range(NU + 1):
                    if u < NU:
                        i, e = divmod(u, E)
                        if e == 0:
                            dve.wait_ge(gates_turned, b * NT + i + 1)
                            dve.tensor_copy(gates_t[:, i % 2, :], gate_bank[0:E, i % 2, 0:P]).then_inc(gates_t_ready, 1)
                        dve.wait_ge(hid_filled, b * NU + u + 1)
                        dve.tensor_tensor(hid[:, u % 2, :], in_bank[:, u % 2, :], b_in_sb[:, e, :],
                                          ALU.add).then_inc(hid_ready, 1)
                    if u >= 1:
                        i, e = divmod(u - 1, E)
                        dve.wait_ge(gated, b * NU + u)
                        if u == 1:
                            dve.wait_ge(turned, b * NU)
                        elif u >= 3:
                            dve.wait_ge(turned, b * NU + u - 2)
                        dve.scalar_tensor_tensor(prod[:, (u - 1) % 2, :], act_g[:, (u - 1) % 2, :],
                                                 gates_now[:, i, e:e + 1], hid[:, (u - 1) % 2, I:2 * I],
                                                 ALU.mult, ALU.mult).then_inc(prod_ready, 1)
                    if u >= 4 and (u - 4) % E == E - 1 or u == NU:
                        i = (u - 4) // E if u < NU else NT - 1
                        dve.wait_ge(summed, b * NT + i + 1)
                        dve.wait_ge(h2_in, b * 16 + 16)
                        dve.wait_ge(saved[i % 2], (b * (NT // 2) + i // 2) * 16)
                        dve.tensor_tensor(res[:, i % 2, :], y_bank[:, i % 2, 0:D], h2[:, i, :],
                                          ALU.add).then_inc(res_ready, 1)

        @block.tensor
        def _(pe):
            pe.wait_ge(w_loaded, 64)
            pe.wait_ge(ident_ready, 1)
            with pe.Fori(0, B) as b:
                pe.wait_ge(xt_in, b * 16 + 16)
                pe.wait_ge(gates_copied, b + 1)
                for u in range(NU + 2):
                    if u < NU:
                        i, e = divmod(u, E)
                        if e == 0:
                            pe.wait_ge(gates_t_ready, b * NT + max(i - 1, 0))
                            pe.transpose(gate_bank[0:E, i % 2, 0:P], gates_now[:, i, :],
                                         ident[:, :]).then_inc(gates_turned, 1)
                        pe.wait_ge(hid_ready, b * NU + max(u - 1, 0))
                        for c in range(DC):
                            last = pe.matmul(in_bank[:, u % 2, :], xt[:, c, i * P:(i + 1) * P], w_in_sb[:, c, e, :],
                                             start=(c == 0), stop=(c == DC - 1))
                        last.then_inc(hid_filled, 1)
                    if 1 <= u <= NU:
                        w = u - 1
                        pe.wait_ge(prod_ready, b * NU + w + 1)
                        pe.wait_ge(prod_t_ready, b * NU + max(w - 1, 0))
                        for c in range(DC):
                            last = pe.transpose(turn_bank[:, w % 2, c * P:(c + 1) * P], prod[:, w % 2, c * P:(c + 1) * P],
                                                ident[:, :])
                        last.then_inc(turned, 1)
                    if u >= 2:
                        w = u - 2
                        i, e = divmod(w, E)
                        pe.wait_ge(prod_t_ready, b * NU + w + 1)
                        if e == 0:
                            pe.wait_ge(res_ready, b * NT + max(i - 1, 0))
                            pe.wait_ge(gates_t_ready, b * NT + i + 1)
                            pe.matmul(y_bank[:, i % 2, 0:D], gates_t[:, i % 2, :], b_out_sb[:, :], start=True, stop=False)
                        for c in range(DC):
                            last = pe.matmul(y_bank[:, i % 2, 0:D], prod_t[:, w % 2, c, :], w_out_sb[:, c, e, :],
                                             start=False, stop=(e == E - 1 and c == DC - 1))
                        if e == E - 1:
                            last.then_inc(summed, 1)


def build(nc, x, wv, bv, wo_t, bo, decay_rev, w_qkv, w_out, router_t, w_in_t, b_in, w_out_t, b_out, out):
    band_dram = nc.dram_tensor("band_dram", (P * 161 + 161,), F32, kind="Internal").ap()
    h2_dram = nc.dram_tensor("h2_dram", (B, P, NT, D), F32, kind="Internal").ap()
    xn2t_dram = nc.dram_tensor("xn2t_dram", (B, P, DC, SP_), F32, kind="Internal").ap()
    with nc.sbuf_tensor("gates", [P, B * NT, E], F32) as gates:
        token_mixer_and_attention(nc, x, wv, bv, wo_t, bo, decay_rev, w_qkv, w_out, router_t,
                                  band_dram, h2_dram, xn2t_dram, gates)
        experts(nc, w_in_t, b_in, w_out_t, b_out, h2_dram, xn2t_dram, gates, out)


def kernel(x, L0_tok_Wv, L0_tok_bv, L0_tok_Wo, L0_tok_bo, L0_tok_decay_w, L0_attn_W_qkv, L0_attn_W_out,
           L0_ffn_router_w, L0_ffn_w_in, L0_ffn_b_in, L0_ffn_w_out, L0_ffn_b_out):
    import numpy as np
    import concourse.bacc as bacc
    from concourse.bass_utils import run_bass_kernel_spmd

    laid_out = {
        "x": x, "wv": L0_tok_Wv, "bv": np.asarray(L0_tok_bv).reshape(DC, P).T, "wo_t": np.asarray(L0_tok_Wo).T, "bo": L0_tok_bo,
        "decay_rev": np.asarray(L0_tok_decay_w)[::-1], "w_qkv": L0_attn_W_qkv, "w_out": L0_attn_W_out,
        "router_t": np.asarray(L0_ffn_router_w).T,
        "w_in_t": np.asarray(L0_ffn_w_in).transpose(2, 0, 1), "b_in": L0_ffn_b_in,
        "w_out_t": np.asarray(L0_ffn_w_out).transpose(2, 0, 1), "b_out": L0_ffn_b_out,
    }
    nc = bacc.Bacc("TRN2", target_bir_lowering=False, num_devices=1)
    arrays, args = {}, []
    for name, a in laid_out.items():
        a = np.ascontiguousarray(a)
        arrays[f"in_{name}"] = a
        args.append(nc.dram_tensor(f"in_{name}", a.shape, mybir.dt.from_np(a.dtype), kind="ExternalInput").ap())
    out = nc.dram_tensor("out", (B, S, D), F32, kind="ExternalOutput").ap()
    build(nc, *args, out)
    r = run_bass_kernel_spmd(nc, [arrays], core_ids=[0])
    return r.results[0]["out"]
```

```python
from contextlib import ExitStack

import concourse.bass as bass
from concourse import mybir

ALU = mybir.AluOpType
ACT = mybir.ActivationFunctionType
AX = mybir.AxisListType
F32 = mybir.dt.float32
F32R = mybir.dt.float32r
BF16 = mybir.dt.bfloat16

P = 128
B, T, D = 8, 750, 256
TAPS = 32
S = T + 1
NT = -(-S // P)
SP_ = NT * P
DC = D // P
H, HD = 16, 16
HC = H // DC
W = 64
NB = SP_ // W
KP = W + SP_
E, I = 8, 256
K = 2
ROWS = B * SP_
REGION = ROWS + P
TILES = ROWS * K // P + E
BIG = 1e30
EPS = 1e-5
SCALE = float(HD) ** -0.5
DVE_STEPS = 25
BANDW = P + TAPS

ACT_FILLS = 3 + 3 + 3 + 3 + 1 + 2 * NB + 3 + 3
DVE_FILLS = 3 + 3 + NT * H // 2 + NT + 3 + 2
RING = 3


def token_mixer_and_attention(nc, x, wv, bv, wo_t, bo, decay_rev, w_qkv, w_out, router_t,
                              band_dram, h2_dram, x_slots, gates, slots, tile_expert, tile_row):
    with ExitStack() as ctx:
        def sb(name, shape, dt=F32):
            return ctx.enter_context(nc.sbuf_tensor(name, shape, dt))

        def sem(name):
            return ctx.enter_context(nc.semaphore(name))

        act_bank = ctx.enter_context(nc.psum_tensor("act_bank", [P, RING, 512], F32))
        dve_bank = ctx.enter_context(nc.psum_tensor("dve_bank", [P, RING, 512], F32))
        out_bank = ctx.enter_context(nc.psum_tensor("out_bank", [P, 2, 512], F32))

        ident = sb("ident", [P, P])
        ident_b = sb("ident_b", [P, P], BF16)
        band = sb("band", [P, BANDW])
        key_mask = sb("key_mask", [P, 2, 2, P + W], BF16)
        query_mask = sb("query_mask", [W + 3, 2, P], BF16)
        half_neg = sb("half_neg", [P, NT])
        decay = sb("decay", [P, TAPS])
        mix_w = sb("mix_w", [P, DC, D])
        bias_h = sb("bias_h", [P, D])
        bv_sb = sb("bv_sb", [P, DC])
        decay_sum = sb("decay_sum", [P, 1])
        bv_sum = sb("bv_sum", [P, DC])
        wqkv_sb = sb("wqkv_sb", [P, DC, 3 * D])
        wout_sb = sb("wout_sb", [P, DC, D])
        rt_sb = sb("rt_sb", [P, DC, E])
        expert_no = sb("expert_no", [P, NT, E])
        before = sb("before", [P, P], BF16)
        ones_b = sb("ones_b", [P, P], BF16)
        row_start = sb("row_start", [P, E])
        region_start = sb("region_start", [P, E])
        tile_no = sb("tile_no", [1, TILES])

        x_sb = sb("x_sb", [P, NT, D])
        st = sb("st", [P, DC, SP_])
        h = sb("h", [P, NT, D])
        xn = sb("xn", [P, NT, D])
        xnt = sb("xnt", [P, DC, SP_])
        qt = sb("qt", [P, DC, SP_])
        qt_r = sb("qt_r", [P, DC, SP_], F32R)
        kt = sb("kt", [P, DC, KP])
        kt_r = sb("kt_r", [P, DC, KP], F32R)
        q_heads = sb("q_heads", [P, DC, HC, SP_])
        k_heads = sb("k_heads", [P, DC, HC // 2, KP], F32R)
        v_a = sb("v_a", [P, NT, H, 2 * HD])
        v_b = sb("v_b", [P, NT, H, 2 * HD])
        qmask_and_max = sb("qmask_and_max", [W + 3, H, SP_], BF16)
        neg_max = sb("neg_max", [P, NT, H])
        max_rest = sb("max_rest", [P, NT, H])
        max_parts = sb("max_parts", [P, NT, 3, H], BF16)
        max_t = sb("max_t", [3 * H, SP_], BF16)
        probs = kt_r[:, :, :].rearrange("p c k -> p (c k)")[:, 0:3 * HC * W].bitcast(F32).rearrange(
            "p (r h q) -> p r h q", r=3, h=HC)
        out_t = sb("out_t", [P, 2, 4, P])
        recip = sb("recip", [P, 2, H])
        wv_sb = xnt[:, :, 0:D]
        bv_wide = xnt[:, :, D:D + P]
        wo_sb = xn[:, 0:DC, :]
        is_choice = st[:, 0, :].rearrange("p (i e) -> p i e", e=E)
        shift_of = st[:, 1, 0:K * B * NT]
        attn = xn[:, :, :].rearrange("p i (h d) -> p i h d", h=H)
        attn_t = xnt[:, :, :]
        h2 = h[:, :, :]
        xn2t = st[:, :, :]
        xn2 = qt[:, :, :].rearrange("p c n -> p (c n)").rearrange("p (i d) -> p i d", d=D)
        zeros = x_sb[:, :, :].rearrange("p i d -> p (i d)")[:, 0:161]
        stats = sb("stats", [P, NT, 6])
        moments = sb("moments", [P, NT, 2])
        var_eps = sb("var_eps", [P, NT])
        rstd = sb("rstd", [P, NT])
        logits = sb("logits", [P, NT, E])
        top_logit = sb("top_logit", [P, NT])
        shifted = sb("shifted", [P, NT, E])
        exps = sb("exps", [P, NT, E])
        exp_sum = sb("exp_sum", [P, NT])
        exp_rec = sb("exp_rec", [P, NT])
        rprobs = sb("rprobs", [P, NT, E])
        best = sb("best", [P, NT, 8])
        best_at = sb("best_at", [P, NT, 8], mybir.dt.uint32)
        best_at_f = sb("best_at_f", [P, NT, 8])
        hot0 = sb("hot0", [P, NT, E])
        hot1 = sb("hot1", [P, NT, E])
        chosen = sb("chosen", [P, NT, E], BF16)
        place = sb("place", [P, NT, E])
        place_k = sb("place_k", [P, K, NT, E])
        slot_f = sb("slot_f", [P, K, NT])
        slot_now = sb("slot_now", [P, K, NT], mybir.dt.uint32)
        count = sb("count", [P, E])
        count_i = sb("count_i", [P, E], mybir.dt.int32)
        tiles_of = sb("tiles_of", [P, E])
        first_tile = sb("first_tile", [P, E + 1])
        to_tile = sb("to_tile", [P, E])
        choice = sb("choice", [P, K, B * NT])
        row_of_choice = sb("row_of_choice", [P, K, B * NT])
        jump = sb("jump", [P, E])
        tile_c = sb("tile_c", [1, TILES])
        xn_row = xn[:, :, :].rearrange("p i d -> p (i d)")
        reached = xn_row[0:1, 0:TILES * (E - 1)].rearrange("p (t e) -> p t e", e=E - 1)
        jumped = xn_row[0:1, TILES * (E - 1):2 * TILES * (E - 1)].rearrange("p (t e) -> p t e", e=E - 1)
        reach_sum = sb("reach_sum", [1, TILES])
        jump_sum = sb("jump_sum", [1, TILES])
        tile_start = sb("tile_start", [1, TILES])
        end_row = sb("end_row", [1, E], mybir.dt.int32)

        weights_in = sem("weights_in")
        small_in = sem("small_in")
        band_zeroed = sem("band_zeroed")
        band_written = sem("band_written")
        band_in = sem("band_in")
        consts_ready = sem("consts_ready")
        zeros_ready = sem("zeros_ready")
        pool_chain = sem("pool_chain")
        dve_passed = sem("dve_passed")
        pe_passed = sem("pe_passed")
        pool_passed = sem("pool_passed")
        sp_passed = sem("sp_passed")
        setup_chain = sem("setup_chain")
        setup_mm = sem("setup_mm")
        mix_ready = sem("mix_ready")
        x_in = sem("x_in")
        conv_done = sem("conv_done")
        act_filled = sem("act_filled")
        act_copied = sem("act_copied")
        dve_filled = sem("dve_filled")
        dve_copied = sem("dve_copied")
        out_copied = sem("out_copied")
        xn_ready = sem("xn_ready")
        dve_chain = sem("dve_chain")
        var_ready = sem("var_ready")
        rstd_ready = sem("rstd_ready")
        q_rounded = sem("q_rounded")
        k_rounded = sem("k_rounded")
        q_placed = sem("q_placed")
        k_placed = sem("k_placed")
        v_shifted = sem("v_shifted")
        parts_ready = sem("parts_ready")
        max_placed = sem("max_placed")
        maxes_done = sem("maxes_done")
        probs_used = sem("probs_used")
        attn_ready = sem("attn_ready")
        h2_saved = sem("h2_saved")
        chosen_ready = sem("chosen_ready")
        slots_ready = sem("slots_ready")
        scattered = sem("scattered")
        ends_ready = sem("ends_ready")
        ends_cleared = sem("ends_cleared")
        rest_zeroed = sem("rest_zeroed")
        shifted_ready = sem("shifted_ready")
        exps_ready = sem("exps_ready")

        def act_free(b, k):
            return b * ACT_FILLS + max(k + 1, RING)

        def act_has(b, k):
            return b * ACT_FILLS + k + 1 + RING

        def dve_free(b, k):
            return b * DVE_FILLS + max(k + 1, RING)

        def dve_has(b, k):
            return b * DVE_FILLS + k + 1 + RING

        def probs_before(b):
            return b * 2 * NB + 3

        A_ST, A_XNT, A_Q, A_V = 0, 3, 6, 9
        A_MAX, A_SC = 12, 13
        A_AT, A_X2 = A_SC + 2 * NB, A_SC + 2 * NB + 3
        D_H, D_K, D_MAX = 0, 3, 6
        D_OUT = D_MAX + NT * H // 2
        D_PROJ, D_ROUTE, D_RANK = D_OUT + NT, D_OUT + NT + 3, D_OUT + NT + 4
        assert A_X2 + 3 == ACT_FILLS and D_RANK + 1 == DVE_FILLS
        N_PLACE = DC * HC * 16

        def thirds(dst, bank, off=0):
            return [(dst[:, 0, off:off + 512], bank[:, 0:512]),
                    (dst[:, 1, off:off + 512], bank[:, 0:512]),
                    (dst[:, 0:2, off + 512:off + SP_], bank[:, 0:512].rearrange("p (c n) -> p c n", c=2))]

        block = ctx.enter_context(nc.Block())

        @block.sync
        def _(sp):
            sp.dma_start(wv_sb[:, :, :], wv.rearrange("(c p) n -> p c n", p=P)).then_inc(weights_in, 16)
            sp.dma_start(wo_sb[:, :, :], wo_t.rearrange("(c p) n -> p c n", p=P)).then_inc(weights_in, 16)
            sp.dma_start(wqkv_sb[:, :, :], w_qkv.rearrange("(c p) n -> p c n", p=P)).then_inc(weights_in, 16)
            sp.dma_start(wout_sb[:, :, :], w_out.rearrange("(c p) n -> p c n", p=P)).then_inc(weights_in, 16)
            sp.dma_start(rt_sb[:, :, :], router_t.rearrange("(c p) n -> p c n", p=P)).then_inc(weights_in, 16)
            sp.wait_ge(zeros_ready, 1)
            sp.dma_start(band_dram[0:P * 161].rearrange("(p j) -> p j", j=161), zeros).then_inc(band_zeroed, 16)
            sp.wait_ge(band_zeroed, 16)
            sp.wait_ge(small_in, 48)
            sp.dma_start(band_dram[1:1 + P * 161].rearrange("(p j) -> p j", j=161)[:, 0:TAPS],
                         decay[:, :]).then_inc(band_written, 16)
            sp.wait_ge(band_written, 16)
            sp.dma_start(band[:, :], band_dram[0:P * BANDW].rearrange("(p j) -> p j", j=BANDW)).then_inc(band_in, 16)
            sp.wait_ge(consts_ready, 17)
            with sp.Fori(0, B) as b:
                sp.wait_ge(act_copied, act_has(b, A_Q + 2))
                sp.wait_ge(probs_used, probs_before(b))
                for c in range(DC):
                    for g in range(HC):
                        sp.dma_start(q_heads[g * HD:(g + 1) * HD, c, g, :],
                                     qt[g * HD:(g + 1) * HD, c, :]).then_inc(q_placed, 16)
                sp.wait_ge(k_rounded, b + 1)
                for c in range(DC):
                    for g in range(HC):
                        sp.dma_start(k_heads[g * HD:(g + 1) * HD, c, g % (HC // 2), :].bitcast(F32),
                                     kt_r[g * HD:(g + 1) * HD, c, :].bitcast(F32)).then_inc(k_placed, 16)
                sp.wait_ge(act_copied, act_has(b, A_V + 2))
                sp.wait_ge(probs_used, probs_before(b))
                sp.dma_start(v_b[W:P, :, :, :], v_a[0:W, :, :, :]).then_inc(v_shifted, 16)
                sp.dma_start(v_b[0:W, 1:NT, :, :], v_a[W:P, 0:NT - 1, :, :]).then_inc(v_shifted, 16)
                sp.wait_ge(act_copied, act_has(b, A_MAX))
                for k in range(3):
                    sp.dma_start(qmask_and_max[W + k:W + k + 1, :, :],
                                 max_t[k * H:(k + 1) * H, :]).then_inc(max_placed, 16)
                sp.wait_ge(dve_copied, dve_has(b, D_PROJ + 2))
                sp.dma_start(h2_dram[b, :, :, :], h2[:, :, :]).then_inc(h2_saved, 16)
                sp.wait_ge(maxes_done, b + 1)
                sp.sem_inc(sp_passed, 1)
            sp.wait_ge(h2_saved, B * 16)
            sp.wait_ge(ends_ready, 1)
            sp.wait_ge(rest_zeroed, 1)
            for e in range(E):
                at = sp.value_load(end_row[0:1, e:e + 1], min_val=e * REGION, max_val=e * REGION + ROWS)
                sp.dma_start(x_slots[bass.ds(at, P), :], x_sb[:, 0, :]).then_inc(ends_cleared, 16)
            sp.wait_ge(ends_cleared, E * 16)

        @block.gpsimd
        def _(pool):
            pool.memset(zeros, 0.0).then_inc(zeros_ready, 1)
            pool.dma_start(decay[:, :], decay_rev.partition_broadcast(P)).then_inc(small_in, 16)
            pool.dma_start(bv_sb[:, :], bv).then_inc(small_in, 16)
            pool.dma_start(bias_h[:, :], bo.partition_broadcast(P)).then_inc(small_in, 16)
            pool.memset(ident[:, :], 1.0).then_inc(pool_chain, 1)
            pool.memset(ident_b[:, :], 1.0).then_inc(pool_chain, 1)
            pool.memset(qmask_and_max[0:W, :, :], 1.0).then_inc(pool_chain, 1)
            pool.memset(query_mask[0:W, :, :], 0.0).then_inc(pool_chain, 1)
            pool.memset(key_mask[:, :, :, :], 0.0).then_inc(pool_chain, 1)
            pool.memset(ones_b[:, :], 1.0).then_inc(pool_chain, 1)
            pool.wait_ge(pool_chain, 6)
            pool.affine_select(ident[:, :], ident[:, :], [[-1, P]], ALU.is_equal, 0.0, base=0,
                               channel_multiplier=1).then_inc(consts_ready, 1)
            pool.affine_select(ident_b[:, :], ident_b[:, :], [[-1, P]], ALU.is_equal, 0.0, base=0,
                               channel_multiplier=1).then_inc(consts_ready, 1)
            im = qmask_and_max[0:W, :, :].rearrange("p h (n w) -> p (h n) w", w=W)
            pool.affine_select(im, im, [[0, H * NB], [-1, W]], ALU.is_equal, 0.0, base=0,
                               channel_multiplier=1).then_inc(consts_ready, 1)
            qm = query_mask[0:W, :, :]
            pool.affine_select(qm, qm, [[0, 2], [1, P]], ALU.is_gt, -BIG, base=0,
                               channel_multiplier=-1).then_inc(pool_chain, 1)
            pool.wait_ge(pool_chain, 7)
            pool.affine_select(qm, qm, [[0, 2], [-1, P]], ALU.is_ge, -BIG, base=W,
                               channel_multiplier=1).then_inc(pool_chain, 1)
            pool.wait_ge(pool_chain, 8)
            qm0 = query_mask[0:W, 0, :]
            pool.affine_select(qm0, qm0, [[1, P]], ALU.is_ge, -BIG, base=-W,
                               channel_multiplier=0).then_inc(consts_ready, 1)
            km = key_mask[:, :, :, :].rearrange("p a b k -> p (a b) k")
            pool.affine_select(km, km, [[0, 4], [1, P + W]], ALU.is_gt, -BIG, base=0,
                               channel_multiplier=-1).then_inc(pool_chain, 1)
            pool.wait_ge(pool_chain, 9)
            pool.affine_select(km, km, [[0, 4], [-1, P + W]], ALU.is_ge, -BIG, base=W,
                               channel_multiplier=1).then_inc(pool_chain, 1)
            pool.wait_ge(pool_chain, 10)
            km0 = key_mask[:, 0, :, :]
            pool.affine_select(km0, km0, [[0, 2], [1, P + W]], ALU.is_ge, -BIG, base=-W,
                               channel_multiplier=0).then_inc(consts_ready, 1)
            pool.memset(half_neg[:, :], -0.5).then_inc(consts_ready, 1)
            pool.memset(q_heads[:, :, :, :], 0.0).then_inc(consts_ready, 1)
            pool.memset(k_heads[:, :, :, :].bitcast(F32), 0.0).then_inc(consts_ready, 1)
            pool.iota(tile_no[:, :], [[1, TILES]], base=0, channel_multiplier=0,
                      allow_small_or_imprecise_dtypes=True).then_inc(consts_ready, 1)
            pool.iota(region_start[:, :], [[REGION, E]], base=0, channel_multiplier=0,
                      allow_small_or_imprecise_dtypes=True).then_inc(consts_ready, 1)
            pool.affine_select(before[:, :], ones_b[:, :], [[1, P]], ALU.is_gt, 0.0, base=0,
                               channel_multiplier=-1).then_inc(consts_ready, 1)
            pool.iota(expert_no[:, :, :], [[0, NT], [1, E]], base=0, channel_multiplier=0,
                      allow_small_or_imprecise_dtypes=True).then_inc(consts_ready, 1)
            pool.wait_ge(consts_ready, 17)
            pool.wait_ge(band_zeroed, 16)
            def load_x(b):
                pool.dma_start(x_sb[:, 0:NT - 1, :],
                               x[b, 0:(NT - 1) * P, :].rearrange("(i p) d -> p i d", p=P)).then_inc(x_in, 16)
                pool.dma_start(x_sb[0:T - (NT - 1) * P, NT - 1, :], x[b, (NT - 1) * P:T, :]).then_inc(x_in, 16)

            def batch(b, more):
                pool.wait_ge(var_ready, 2 * b + 1)
                pool.tensor_tensor(rstd[:, :], var_eps[:, :], half_neg[:, :], ALU.pow).then_inc(rstd_ready, 1)
                if more:
                    pool.wait_ge(conv_done, b + 1)
                    load_x(b + 1)
                pool.wait_ge(act_copied, act_has(b, A_Q + 2))
                pool.sem_inc(pool_passed, 1)
                pool.tensor_copy(qt_r[:, :, :], qt[:, :, :]).then_inc(q_rounded, 1)
                pool.wait_ge(dve_copied, dve_has(b, D_K + 2))
                pool.sem_inc(pool_passed, 1)
                pool.tensor_copy(kt_r[:, :, :], kt[:, :, :]).then_inc(k_rounded, 1)
                pool.wait_ge(var_ready, 2 * b + 2)
                pool.tensor_tensor(rstd[:, :], var_eps[:, :], half_neg[:, :], ALU.pow).then_inc(rstd_ready, 1)
                pool.wait_ge(slots_ready, b + 1)
                pool.sem_inc(pool_passed, 1)
                for k in range(K):
                    for i in range(NT):
                        pool.indirect_dma_start(
                            out=x_slots, out_offset=bass.IndirectOffsetOnAxis(ap=slot_now[:, k, i:i + 1], axis=0),
                            in_=xn2[:, i, :], in_offset=None).then_inc(scattered, 16)
                pool.wait_ge(k_placed, (b + 1) * N_PLACE)

            load_x(0)
            with pool.Fori(0, B - 1) as b:
                batch(b, True)
            batch(B - 1, False)
            pool.wait_ge(scattered, B * K * NT * 16)
            pool.wait_ge(conv_done, B)
            pool.memset(x_sb[:, 0, :], 0.0).then_inc(rest_zeroed, 1)

        @block.scalar
        def _(act):
            act.wait_ge(setup_mm, 1)
            act.copy(mix_w[:, :, :], act_bank[:, 0, :].rearrange("p (c n) -> p c n", c=DC)).then_inc(mix_ready, 1)
            act.wait_ge(mix_ready, 1)
            act.sem_inc(act_copied, RING)
            with act.Fori(0, B) as b:
                def bank(k):
                    return act_bank[:, (A0 + k) % RING, :]
                A0 = 0

                def fill(k):
                    act.wait_ge(act_filled, b * ACT_FILLS + k + 1)

                for k in range(3):
                    fill(A_ST + k)
                    d, s = thirds(st, bank(A_ST + k))[k]
                    act.copy(d, s).then_inc(act_copied, 1)
                for k in range(3):
                    fill(A_XNT + k)
                    d, s = thirds(xnt, bank(A_XNT + k))[k]
                    act.copy(d, s).then_inc(act_copied, 1)
                for k in range(3):
                    fill(A_Q + k)
                    d, s = thirds(qt, bank(A_Q + k))[k]
                    act.mul(d, s, SCALE).then_inc(act_copied, 1)
                for k in range(3):
                    fill(A_V + k)
                    act.copy(v_a[:, 2 * k:2 * k + 2, :, 0:HD],
                             bank(A_V + k).rearrange("p (i h d) -> p i h d", i=2, h=H)).then_inc(act_copied, 1)
                fill(A_MAX)
                act.copy(max_t[:, :], bank(A_MAX).bitcast(BF16)[0:3 * H, 0:SP_]).then_inc(act_copied, 1)
                for n in range(2 * NB):
                    fill(A_SC + n)
                    act.wait_ge(probs_used, b * 2 * NB + n + 1)
                    act.activation(probs[:, n % 3, :, :], bank(A_SC + n).rearrange("p (h q) -> p h q", h=HC),
                                   ACT.Exp).then_inc(act_copied, 1)
                for k in range(3):
                    fill(A_AT + k)
                    d, s = thirds(attn_t, bank(A_AT + k))[k]
                    act.copy(d, s).then_inc(act_copied, 1)
                for k in range(3):
                    fill(A_X2 + k)
                    d, s = thirds(xn2t, bank(A_X2 + k))[k]
                    act.copy(d, s).then_inc(act_copied, 1)
                act.wait_ge(shifted_ready, b + 1)
                act.activation(exps[:, :, :], shifted[:, :, :], ACT.Exp).then_inc(exps_ready, 1)
                act.wait_ge(q_placed, (b + 1) * N_PLACE)
                act.wait_ge(q_rounded, b + 1)
                act.wait_ge(v_shifted, (b + 1) * 32)
                act.wait_ge(max_placed, (b + 1) * 48)
                act.wait_ge(scattered, (b + 1) * K * NT * 16)

        @block.vector
        def _(dve):
            chain = [0]

            def step(ins, base, n):
                chain[0] += 1
                ins.then_inc(dve_chain, 1)
                dve.wait_ge(dve_chain, base + chain[0])

            dve.memset(query_mask[W:W + 3, :, :], 1.0).then_inc(consts_ready, 1)
            dve.memset(x_sb[96:P, NT - 1, :], 0.0).then_inc(consts_ready, 1)
            dve.memset(v_a[:, :, :, HD:2 * HD], 1.0).then_inc(consts_ready, 1)
            dve.memset(v_b[0:W, 0, :, :], 0.0).then_inc(consts_ready, 1)
            dve.memset(kt[:, :, 0:W], 0.0).then_inc(consts_ready, 1)
            dve.wait_ge(small_in, 48)
            dve.tensor_reduce(decay_sum[:, :], decay[:, :], AX.X, ALU.add).then_inc(setup_chain, 1)
            dve.wait_ge(setup_chain, 1)
            dve.tensor_scalar(bv_sum[:, :], bv_sb[:, :], decay_sum[:, 0:1], None, ALU.mult).then_inc(setup_chain, 1)
            dve.wait_ge(setup_chain, 2)
            dve.tensor_copy(bv_wide[:, :, :], bv_sum[:, :].unsqueeze(2).to_broadcast([P, DC, P])).then_inc(setup_chain, 1)
            dve.wait_ge(setup_mm, 2)
            dve.tensor_tensor(bias_h[:, :], dve_bank[:, 0, 0:D], bias_h[:, :], ALU.add).then_inc(dve_copied, RING)
            dve.sem_inc(out_copied, 2)
            dve.wait_ge(dve_copied, RING)
            dve.wait_ge(consts_ready, 17)
            dve.tensor_copy(row_start[:, :], region_start[:, :])
            with dve.Fori(0, B) as b:
                base = b * DVE_STEPS
                chain[0] = 0

                def st_(ins):
                    step(ins, base, 0)

                def bank(k):
                    return dve_bank[:, k % RING, :]

                def fill(k):
                    dve.wait_ge(dve_filled, b * DVE_FILLS + k + 1)

                def layer_norm(src, dst, pass_no):
                    for i in range(NT):
                        last = dve.bn_stats(stats[:, i, :], src[:, i, :])
                    st_(last)
                    dve.sem_inc(dve_passed, 1)
                    for i in range(NT):
                        last = dve.bn_aggr(moments[:, i, :], stats[:, i, :])
                    st_(last)
                    dve.tensor_scalar(var_eps[:, :], moments[:, :, 1], EPS, None, ALU.add).then_inc(var_ready, 1)
                    dve.wait_ge(rstd_ready, 2 * b + 1 + pass_no)
                    for i in range(NT):
                        dve.tensor_scalar(dst[:, i, :], src[:, i, :], moments[:, i, 0:1], rstd[:, i:i + 1],
                                          ALU.subtract, ALU.mult).then_inc(xn_ready, 1)

                for k in range(3):
                    fill(D_H + k)
                    last = dve.tensor_tensor(h[:, 2 * k:2 * k + 2, :],
                                             bank(D_H + k).rearrange("p (i d) -> p i d", i=2),
                                             bias_h[:, :].unsqueeze(1).to_broadcast([P, 2, D]), ALU.add)
                    last.then_inc(dve_copied, 1)
                dve.wait_ge(dve_copied, dve_has(b, D_H + 2))
                layer_norm(h, xn, 0)
                for k in range(3):
                    fill(D_K + k)
                    d, s = thirds(kt, bank(D_K + k), W)[k]
                    dve.tensor_copy(d, s).then_inc(dve_copied, 1)
                for n in range(NT * H // 2):
                    i, g = divmod(n, H // 2)
                    fill(D_MAX + n)
                    dve.tensor_reduce(neg_max[:, i, 2 * g:2 * g + 2],
                                      bank(D_MAX + n)[:, 0:2 * (P + W)].rearrange("p (h k) -> p h k", h=2),
                                      AX.X, ALU.max, negate=True).then_inc(dve_copied, 1)
                dve.wait_ge(dve_copied, dve_has(b, D_OUT - 1))
                st_(dve.tensor_copy(max_parts[:, :, 0, :], neg_max[:, :, :]))
                st_(dve.tensor_tensor(max_rest[:, :, :], neg_max[:, :, :], max_parts[:, :, 0, :], ALU.subtract))
                st_(dve.tensor_copy(max_parts[:, :, 1, :], max_rest[:, :, :]))
                st_(dve.tensor_tensor(max_rest[:, :, :], max_rest[:, :, :], max_parts[:, :, 1, :], ALU.subtract))
                dve.tensor_copy(max_parts[:, :, 2, :], max_rest[:, :, :]).then_inc(parts_ready, 1)
                for i in range(NT + 1):
                    if i < NT:
                        dve.wait_ge(probs_used, probs_before(b) + 4 * (i + 1))
                        dve.tensor_copy(out_t[:, i % 2, :, :],
                                        out_bank[:, i % 2, :].rearrange("p (g q) -> p g q", g=4)).then_inc(out_copied, 1)
                    if i >= 1:
                        j = i - 1
                        fill(D_OUT + j)
                        back = bank(D_OUT + j).rearrange("p (h d) -> p h d", d=2 * HD)
                        st_(dve.reciprocal(recip[:, j % 2, :], back[:, :, HD]))
                        dve.tensor_tensor(attn[:, j, :, :], back[:, :, 0:HD],
                                          recip[:, j % 2, :].unsqueeze(2).to_broadcast([P, H, HD]),
                                          ALU.mult).then_inc(dve_copied, 1)
                for k in range(3):
                    fill(D_PROJ + k)
                    dve.tensor_tensor(h2[:, 2 * k:2 * k + 2, :],
                                      bank(D_PROJ + k).rearrange("p (i d) -> p i d", i=2),
                                      h[:, 2 * k:2 * k + 2, :], ALU.add).then_inc(dve_copied, 1)
                dve.wait_ge(dve_copied, dve_has(b, D_PROJ + 2))
                dve.wait_ge(q_rounded, b + 1)
                dve.wait_ge(q_placed, (b + 1) * N_PLACE)
                layer_norm(h2, xn2, 1)
                fill(D_ROUTE)
                dve.tensor_copy(logits[:, :, :],
                                bank(D_ROUTE)[:, 0:NT * E].rearrange("p (i e) -> p i e", e=E)).then_inc(dve_copied, 1)
                dve.wait_ge(dve_copied, dve_has(b, D_ROUTE))
                st_(dve.tensor_reduce(top_logit[:, :], logits[:, :, :], AX.X, ALU.max))
                dve.tensor_tensor(shifted[:, :, :], logits[:, :, :],
                                  top_logit[:, :].unsqueeze(2).to_broadcast([P, NT, E]),
                                  ALU.subtract).then_inc(shifted_ready, 1)
                dve.wait_ge(exps_ready, b + 1)
                st_(dve.tensor_reduce(exp_sum[:, :], exps[:, :, :], AX.X, ALU.add))
                st_(dve.reciprocal(exp_rec[:, :], exp_sum[:, :]))
                st_(dve.tensor_tensor(rprobs[:, :, :], exps[:, :, :],
                                      exp_rec[:, :].unsqueeze(2).to_broadcast([P, NT, E]), ALU.mult))
                dve.sem_inc(dve_passed, 1)
                for i in range(NT):
                    last = dve.max(best[:, i, :], rprobs[:, i, :])
                st_(last)
                dve.sem_inc(dve_passed, 1)
                for i in range(NT):
                    last = dve.max_index(best_at[:, i, :], best[:, i, :], rprobs[:, i, :])
                st_(last)
                st_(dve.tensor_copy(best_at_f[:, :, :], best_at[:, :, :]))
                dve.tensor_tensor(hot0[:, :, :], expert_no[:, :, :],
                                  best_at_f[:, :, 0:1].to_broadcast([P, NT, E]), ALU.is_equal)
                st_(dve.tensor_tensor(hot1[:, :, :], expert_no[:, :, :],
                                      best_at_f[:, :, 1:2].to_broadcast([P, NT, E]), ALU.is_equal))
                dve.tensor_tensor(chosen[:, :, :], hot0[:, :, :], hot1[:, :, :], ALU.add).then_inc(chosen_ready, 1)
                dve.tensor_copy(gates[:, bass.ts(b, NT), :], best[:, :, 0:K])
                fill(D_RANK)
                rank = bank(D_RANK)[:, 0:NT * E].rearrange("p (i e) -> p i e", e=E)
                st_(dve.tensor_tensor(place[:, :, :], rank,
                                      row_start[:, :].unsqueeze(1).to_broadcast([P, NT, E]), ALU.add))
                dve.tensor_tensor(row_start[:, :], row_start[:, :], bank(D_RANK)[:, NT * E:NT * E + E],
                                  ALU.add).then_inc(dve_copied, 1)
                dve.tensor_tensor(place_k[:, 0, :, :], place[:, :, :], hot0[:, :, :], ALU.mult)
                st_(dve.tensor_tensor(place_k[:, 1, :, :], place[:, :, :], hot1[:, :, :], ALU.mult))
                st_(dve.tensor_reduce(slot_f[:, :, :], place_k[:, :, :, :], AX.X, ALU.add))
                dve.tensor_copy(row_of_choice[:, :, bass.ts(b, NT)], slot_f[:, :, :])
                for k in range(K):
                    dve.tensor_copy(choice[:, k, bass.ts(b, NT)], best_at_f[:, :, k])
                dve.tensor_copy(slot_now[:, :, :], slot_f[:, :, :]).then_inc(slots_ready, 1)
                dve.wait_ge(h2_saved, (b + 1) * 16)
                dve.wait_ge(k_rounded, b + 1)
                dve.wait_ge(scattered, (b + 1) * K * NT * 16)
                assert chain[0] == DVE_STEPS, chain[0]

            end_chain = [0]

            def last_(ins):
                end_chain[0] += 1
                ins.then_inc(setup_chain, 1)
                dve.wait_ge(setup_chain, 3 + end_chain[0])

            dve.wait_ge(dve_copied, RING + B * DVE_FILLS)
            dve.tensor_copy(end_row[:, :], row_start[0:1, :]).then_inc(ends_ready, 1)
            last_(dve.tensor_tensor(count[:, :], row_start[:, :], region_start[:, :], ALU.subtract))
            last_(dve.tensor_scalar(count[:, :], count[:, :], float(P - 1), None, ALU.add))
            last_(dve.tensor_copy(count_i[:, :], count[:, :]))
            last_(dve.tensor_scalar(count_i[:, :], count_i[:, :], P.bit_length() - 1, None, ALU.arith_shift_right))
            last_(dve.tensor_copy(tiles_of[:, :], count_i[:, :]))
            last_(dve.memset(first_tile[:, 0:1], 0.0))
            for e in range(E):
                last_(dve.tensor_tensor(first_tile[:, e + 1:e + 2], first_tile[:, e:e + 1], tiles_of[:, e:e + 1], ALU.add))
            last_(dve.tensor_scalar(count[:, 0:1], first_tile[:, E:E + 1], -1.0, None, ALU.add))
            last_(dve.tensor_scalar(tile_c[:, :], tile_no[:, :], count[0:1, 0:1], None, ALU.min))
            last_(dve.tensor_scalar(jump[:, :], tiles_of[:, :], -float(P), float(REGION), ALU.mult, ALU.add))
            last_(dve.tensor_tensor(reached[:, :, :], tile_c[:, :].unsqueeze(2).to_broadcast([1, TILES, E - 1]),
                                    first_tile[0:1, 1:E].unsqueeze(1).to_broadcast([1, TILES, E - 1]), ALU.is_ge))
            last_(dve.tensor_tensor(jumped[:, :, :], reached[:, :, :],
                                    jump[0:1, 0:E - 1].unsqueeze(1).to_broadcast([1, TILES, E - 1]), ALU.mult))
            last_(dve.tensor_reduce(reach_sum[:, :], reached[:, :, :], AX.X, ALU.add))
            last_(dve.tensor_reduce(jump_sum[:, :], jumped[:, :, :], AX.X, ALU.add))
            last_(dve.tensor_scalar(tile_start[:, :], tile_c[:, :], float(P), None, ALU.mult))
            last_(dve.tensor_tensor(jump_sum[:, :], jump_sum[:, :], tile_start[:, :], ALU.add))
            dve.tensor_copy(tile_expert[:, :], reach_sum[:, :])
            last_(dve.tensor_scalar(to_tile[:, :], first_tile[:, 0:E], float(P), None, ALU.mult))
            last_(dve.tensor_tensor(to_tile[:, :], to_tile[:, :], region_start[:, :], ALU.subtract))
            last_(dve.tensor_tensor(is_choice, expert_no[:, 0:1, :].to_broadcast([P, K * B * NT, E]),
                                    choice[:, :, :].rearrange("p k i -> p (k i)").unsqueeze(2).to_broadcast([P, K * B * NT, E]),
                                    ALU.is_equal))
            last_(dve.tensor_tensor(is_choice, is_choice,
                                    to_tile[:, :].unsqueeze(1).to_broadcast([P, K * B * NT, E]), ALU.mult))
            last_(dve.tensor_reduce(shift_of, is_choice, AX.X, ALU.add))
            dve.tensor_tensor(slots[:, :, :].rearrange("p k i -> p (k i)"),
                              row_of_choice[:, :, :].rearrange("p k i -> p (k i)"), shift_of, ALU.add)
            last_(dve.tensor_copy(tile_row[:, :], jump_sum[:, :]))

        @block.tensor
        def _(pe):
            pe.wait_ge(weights_in, 80)
            pe.wait_ge(setup_chain, 3)
            for m in range(DC):
                for c in range(DC):
                    last = pe.matmul(act_bank[:, 0, m * D:(m + 1) * D], wv_sb[:, c, m * P:(m + 1) * P],
                                     wo_sb[:, c, :], start=(c == 0), stop=(c == DC - 1))
            last.then_inc(setup_mm, 1)
            for c in range(DC):
                last = pe.matmul(dve_bank[:, 0, 0:D], bv_wide[:, c, :], wo_sb[:, c, :],
                                 start=(c == 0), stop=(c == DC - 1))
            last.then_inc(setup_mm, 1)
            pe.sem_inc(probs_used, 3)
            pe.wait_ge(band_in, 16)
            pe.wait_ge(consts_ready, 17)
            with pe.Fori(0, B) as b:
                def act_open(k):
                    pe.wait_ge(act_copied, act_free(b, k))
                    return act_bank[:, k % RING, :]

                def dve_open(k):
                    pe.wait_ge(dve_copied, dve_free(b, k))
                    return dve_bank[:, k % RING, :]

                def product(out, stationary, moving):
                    for c in range(DC):
                        last = pe.matmul(out, stationary(c), moving(c), start=(c == 0), stop=(c == DC - 1))
                    return last

                def project(open_, filled, k0, weight, src):
                    for k in range(3):
                        bk = open_(k0 + k)
                        if k < 2:
                            last = product(bk[:, 0:512], lambda c: weight(c, k), lambda c: src[:, c, 0:512])
                        else:
                            for m in range(2):
                                last = product(bk[:, m * 256:(m + 1) * 256], lambda c: weight(c, m),
                                               lambda c: src[:, c, 512:SP_])
                        last.then_inc(filled, 1)

                def turn(k0, src, ready=None):
                    got = 0
                    for k in range(3):
                        bk = act_open(k0 + k)
                        for j in range(4):
                            c, i = (k, j) if k < 2 else (j // 2, 4 + j % 2)
                            if ready is not None and i + 1 > got:
                                got = i + 1
                                ready(got)
                            last = pe.transpose(bk[:, j * P:(j + 1) * P], src[:, i, c * P:(c + 1) * P], ident[:, :])
                        last.then_inc(act_filled, 1)

                pe.wait_ge(x_in, b * 32 + 32)
                for c in range(DC):
                    bk = act_open(A_ST + c)
                    for i in range(4):
                        n = min(BANDW, 512 - i * P)
                        last = pe.matmul(bk[:, i * P:i * P + n], x_sb[:, i, c * P:(c + 1) * P], band[:, 0:n],
                                         start=(i == 0), stop=(i == 3), skip_group_check=True)
                    last.then_inc(act_filled, 1)
                bk = act_open(A_ST + 2)
                for c in range(DC):
                    o = c * 256
                    pe.matmul(bk[:, o:o + TAPS], x_sb[:, 3, c * P:(c + 1) * P], band[:, P:BANDW],
                              start=True, stop=False, skip_group_check=True)
                    for i in range(4, 6):
                        n = min(BANDW, SP_ - i * P)
                        a = o + (i - 4) * P
                        last = pe.matmul(bk[:, a:a + n], x_sb[:, i, c * P:(c + 1) * P], band[:, 0:n],
                                         start=False, stop=(i == 5), skip_group_check=True)
                last.then_inc(act_filled, 1)
                for k in range(3):
                    bk = dve_open(D_H + k)
                    if k == 0:
                        pe.wait_ge(mix_ready, 1)
                        pe.wait_ge(act_copied, act_has(b, A_ST + 1))
                    if k == 2:
                        pe.wait_ge(act_copied, act_has(b, A_ST + 2))
                    for j in range(2):
                        i = 2 * k + j
                        for c in range(DC):
                            last = pe.matmul(bk[:, j * D:(j + 1) * D], st[:, c, i * P:(i + 1) * P], mix_w[:, c, :],
                                             start=(c == 0), stop=(c == DC - 1))
                            if (i, c) == (0, 0):
                                last.then_inc(conv_done, 1)
                    last.then_inc(dve_filled, 1)
                turn(A_XNT, xn, lambda n: pe.wait_ge(xn_ready, 2 * b * NT + n))
                pe.wait_ge(act_copied, act_has(b, A_XNT + 2))
                project(act_open, act_filled, A_Q, lambda c, m: wqkv_sb[:, c, m * P:(m + 1) * P], xnt)
                project(dve_open, dve_filled, D_K, lambda c, m: wqkv_sb[:, c, D + m * P:D + (m + 1) * P], xnt)
                for k in range(3):
                    bk = act_open(A_V + k)
                    for j in range(2):
                        i = 2 * k + j
                        last = product(bk[:, j * D:(j + 1) * D], lambda c: xnt[:, c, i * P:(i + 1) * P],
                                       lambda c: wqkv_sb[:, c, 2 * D:3 * D])
                    last.then_inc(act_filled, 1)
                pe.wait_ge(q_rounded, b + 1)
                pe.wait_ge(k_placed, (b + 1) * N_PLACE)
                for i in range(NT):
                    for g in range(H // 2):
                        n = i * H // 2 + g
                        c, a = divmod(2 * g, HC)
                        bk = dve_open(D_MAX + n)[:, 0:2 * (P + W)]
                        pe.matmul(bk, ident_b[:, :], key_mask[:, min(i, 1), :, :].rearrange("p h k -> p (h k)"),
                                  start=True, stop=False)
                        half, a = divmod(a, HC // 2)
                        rows = slice(half * W, (half + 1) * W)
                        last = pe.matmul(bk.rearrange("p (h k) -> p h k", h=2), qt_r[rows, c, i * P:(i + 1) * P],
                                         k_heads[rows, c, a:a + 2, i * P:i * P + P + W], start=False, stop=True)
                        last.then_inc(dve_filled, 1)
                pe.wait_ge(parts_ready, b + 1)
                bk = act_open(A_MAX).bitcast(BF16)
                pe.sem_inc(pe_passed, 1)
                for i in range(NT):
                    last = pe.transpose(bk[0:3 * H, i * P:(i + 1) * P],
                                        max_parts[:, i, :, :].rearrange("p a h -> p (a h)"), ident_b[:, :])
                    if i == 0:
                        last.then_inc(maxes_done, 1)
                last.then_inc(act_filled, 1)
                pe.wait_ge(max_placed, (b + 1) * 48)
                pe.wait_ge(q_placed, (b + 1) * N_PLACE)

                def scores(n, c):
                    bk = act_open(A_SC + 2 * n + c).rearrange("p (h q) -> p h q", h=HC)
                    pe.matmul(bk, query_mask[:, min(n, 1), :],
                              qmask_and_max[:, c * HC:(c + 1) * HC, n * W:(n + 1) * W], start=True, stop=False)
                    pe.matmul(bk, kt[:, c, n * W:n * W + P], q_heads[:, c, :, n * W:(n + 1) * W],
                              start=False, stop=True).then_inc(act_filled, 1)

                def values(n, c):
                    pe.wait_ge(act_copied, act_has(b, A_SC + 2 * n + c))
                    if n % 2 == 0 and c == 0:
                        pe.wait_ge(out_copied, b * NT + n // 2 + 1)
                    v = v_b[:, n // 2, :, :] if n % 2 == 0 else v_a[:, n // 2, :, :]
                    for a in range(HC):
                        g, r = divmod(c * HC + a, 4)
                        q0 = g * P + (n % 2) * W
                        last = pe.matmul(out_bank[32 * r:32 * r + 32, (n // 2) % 2, q0:q0 + W],
                                         v[:, c * HC + a, :], probs[:, (2 * n + c) % 3, a, :],
                                         start=True, stop=True)
                    return last

                def out_back(i):
                    pe.wait_ge(out_copied, b * NT + i + 1 + 2)
                    bk = dve_open(D_OUT + i)
                    for g in range(4):
                        last = pe.transpose(bk[:, g * P:(g + 1) * P], out_t[:, i % 2, g, :], ident[:, :])
                    last.then_inc(dve_filled, 1)

                pe.wait_ge(v_shifted, (b + 1) * 32)
                for m in range(2 * NB + 2):
                    if m < 2 * NB:
                        scores(*divmod(m, 2))
                    if m >= 2:
                        n, c = divmod(m - 2, 2)
                        last = values(n, c)
                        last.then_inc(probs_used, 1)
                        if n % 2 == 1 and c == 0 and n >= 3:
                            out_back(n // 2 - 1)
                out_back(NT - 1)
                pe.wait_ge(dve_copied, dve_has(b, D_OUT + NT - 1))
                turn(A_AT, attn[:, :, :, :].rearrange("p i h d -> p i (h d)"))
                for k in range(3):
                    bk = dve_open(D_PROJ + k)
                    pe.wait_ge(act_copied, act_has(b, A_AT + 1 if k < 2 else A_AT + 2))
                    for j in range(2):
                        i = 2 * k + j
                        last = product(bk[:, j * D:(j + 1) * D], lambda c: attn_t[:, c, i * P:(i + 1) * P],
                                       lambda c: wout_sb[:, c, :])
                    last.then_inc(dve_filled, 1)
                turn(A_X2, xn2, lambda n: pe.wait_ge(xn_ready, (2 * b + 1) * NT + n))
                pe.wait_ge(act_copied, act_has(b, A_X2 + 2))
                bk = dve_open(D_ROUTE)
                for i in range(NT):
                    last = product(bk[:, i * E:(i + 1) * E], lambda c: xn2t[:, c, i * P:(i + 1) * P],
                                   lambda c: rt_sb[:, c, :])
                last.then_inc(dve_filled, 1)
                bk = dve_open(D_RANK)
                pe.wait_ge(chosen_ready, b + 1)
                pe.matmul(bk[:, 0:NT * E], before[:, :], chosen[:, :, :].rearrange("p i e -> p (i e)"),
                          start=True, stop=False, skip_group_check=True)
                for k in range(1, NT):
                    pe.matmul(bk[:, k * E:NT * E], ones_b[:, :], chosen[:, 0:NT - k, :].rearrange("p i e -> p (i e)"),
                              start=False, stop=(k == NT - 1), skip_group_check=True)
                for i in range(NT):
                    last = pe.matmul(bk[:, NT * E:NT * E + E], ones_b[:, :], chosen[:, i, :],
                                     start=False, stop=(i == NT - 1), skip_group_check=True)
                last.then_inc(dve_filled, 1)


def experts(nc, w_in_t, b_in, w_out_t, b_out, x_slots, y_slots, tile_expert, tile_row):
    with ExitStack() as ctx:
        def sb(name, shape, dt=F32):
            return ctx.enter_context(nc.sbuf_tensor(name, shape, dt))

        def sem(name):
            return ctx.enter_context(nc.semaphore(name))

        in_bank = ctx.enter_context(nc.psum_tensor("in_bank", [P, 2, 512], F32))
        row_bank = ctx.enter_context(nc.psum_tensor("row_bank", [P, 2, 512], F32))
        turn_bank = ctx.enter_context(nc.psum_tensor("turn_bank", [P, 2, 512], F32))
        y_bank = ctx.enter_context(nc.psum_tensor("y_bank", [P, 2, 512], F32))

        ident = sb("ident2", [P, P])
        w_in_sb = sb("w_in_sb", [P, DC, E, 2 * I])
        w_out_sb = sb("w_out_sb", [P, DC, E, D])
        b_in_sb = sb("b_in_sb", [P, E, 2 * I])
        b_out_sb = sb("b_out_sb", [P, E, D])
        rows = sb("rows", [P, 4, D])
        rows_t = sb("rows_t", [P, 2, DC, P])
        hid = sb("hid", [P, 2, 2 * I])
        act_g = sb("act_g", [P, 2, I])
        prod = sb("prod", [P, 2, I])
        prod_t = sb("prod_t", [P, 2, DC, P])
        y = sb("y", [P, 2, D])

        w_loaded = sem("w_loaded")
        ident_ready = sem("ident_ready")
        ones_ready = sem("ones_ready")
        rows_in = [sem(f"rows_in_{k}") for k in range(4)]
        rows_turned = sem("rows_turned")
        rows_t_ready = sem("rows_t_ready")
        hid_filled = sem("hid_filled")
        hid_ready = sem("hid_ready")
        gated = sem("gated")
        prod_ready = sem("prod_ready")
        turned = sem("turned")
        prod_t_ready = sem("prod_t_ready")
        summed = sem("summed")
        y_ready = sem("y_ready")
        saved = [sem("saved_0"), sem("saved_1")]

        def expert_of(eng, t):
            return eng.value_load(tile_expert[0:1, bass.ds(t, 1)], min_val=0, max_val=E - 1)

        def row_of(eng, t):
            return eng.value_load(tile_row[0:1, bass.ds(t, 1)], min_val=0, max_val=(E - 1) * REGION + ROWS)

        block = ctx.enter_context(nc.Block())

        @block.sync
        def _(sp):
            sp.dma_start(w_in_sb[:, :, :, :], w_in_t.rearrange("(c p) e n -> p c e n", p=P)).then_inc(w_loaded, 16)
            sp.dma_start(w_out_sb[:, :, :, :], w_out_t.rearrange("(c p) e n -> p c e n", p=P)).then_inc(w_loaded, 16)
            sp.dma_start(b_in_sb[:, :, :], b_in.rearrange("e n -> (e n)").partition_broadcast(P)).then_inc(w_loaded, 16)
            sp.dma_start(b_out_sb[:, :, :], b_out.rearrange("e n -> (e n)").partition_broadcast(P)).then_inc(w_loaded, 16)

            def load(t, k):
                sp.dma_start(rows[:, k, :], x_slots[bass.ds(row_of(sp, t), P), :]).then_inc(rows_in[k], 16)

            for k in range(4):
                load(k, k)
            with sp.Fori(0, TILES // 4 - 1) as j:
                for k in range(4):
                    sp.wait_ge(rows_turned, j * 4 + k + 1)
                    load(j * 4 + 4 + k, k)

        @block.gpsimd
        def _(pool):
            pool.memset(ident[:, :], 1.0).then_inc(ones_ready, 1)
            pool.wait_ge(ones_ready, 1)
            pool.affine_select(ident[:, :], ident[:, :], [[-1, P]], ALU.is_equal, 0.0, base=0,
                               channel_multiplier=1).then_inc(ident_ready, 1)
            with pool.Fori(0, TILES // 2) as j:
                for k in range(2):
                    pool.wait_ge(y_ready, j * 2 + k + 1)
                    pool.dma_start(y_slots[bass.ds(j * 2 * P + k * P, P), :], y[:, k, :]).then_inc(saved[k], 16)
            for one in saved:
                pool.wait_ge(one, TILES // 2 * 16)

        @block.scalar
        def _(act):
            def turn_rows(t, k):
                act.wait_ge(rows_turned, t + 1)
                act.copy(rows_t[:, k, :, :],
                         row_bank[:, k, 0:256].rearrange("p (c n) -> p c n", c=2)).then_inc(rows_t_ready, 1)

            turn_rows(0, 0)
            turn_rows(1, 1)

            def step(t, k):
                act.wait_ge(hid_ready, t + 1)
                act.activation(act_g[:, k, :], hid[:, k, 0:I], ACT.Silu).then_inc(gated, 1)
                act.wait_ge(turned, t + 1)
                act.copy(prod_t[:, k, :, :],
                         turn_bank[:, k, 0:256].rearrange("p (c n) -> p c n", c=2)).then_inc(prod_t_ready, 1)

            with act.Fori(0, TILES // 2 - 1) as j:
                for k in range(2):
                    step(j * 2 + k, k)
                    turn_rows(j * 2 + k + 2, k)
            for k in range(2):
                step(TILES - 2 + k, k)

        @block.vector
        def _(dve):
            dve.wait_ge(w_loaded, 64)

            def add_b_in(t, k):
                e = expert_of(dve, t)
                dve.wait_ge(hid_filled, t + 1)
                dve.tensor_tensor(hid[:, k, :], in_bank[:, k, :], b_in_sb[:, bass.ds(e, 1), :], ALU.add).then_inc(hid_ready, 1)

            def step(t, k, y_saved, more=True):
                dve.wait_ge(gated, t + 1)
                dve.tensor_tensor(prod[:, k, :], act_g[:, k, :], hid[:, k, I:2 * I], ALU.mult).then_inc(prod_ready, 1)
                if more:
                    add_b_in(t + 1, 1 - k)
                e = expert_of(dve, t)
                dve.wait_ge(summed, t + 1)
                if y_saved is not None:
                    dve.wait_ge(saved[k], y_saved)
                dve.tensor_tensor(y[:, k, :], y_bank[:, k, 0:D], b_out_sb[:, bass.ds(e, 1), :], ALU.add).then_inc(y_ready, 1)
            add_b_in(0, 0)
            for k in range(2):
                step(k, k, None)
            with dve.Fori(1, TILES // 2 - 1) as j:
                for k in range(2):
                    step(j * 2 + k, k, j * 16)
            for k in range(2):
                step(TILES - 2 + k, k, (TILES // 2 - 1) * 16, more=(k == 0))

        @block.tensor
        def _(pe):
            pe.wait_ge(w_loaded, 64)
            pe.wait_ge(ident_ready, 1)

            def turn_rows(t, k4, arrivals):
                pe.wait_ge(rows_in[k4], arrivals)
                for c in range(DC):
                    last = pe.transpose(row_bank[:, k4 % 2, c * P:(c + 1) * P], rows[:, k4, c * P:(c + 1) * P], ident[:, :])
                last.then_inc(rows_turned, 1)

            def widen(t, k):
                e = expert_of(pe, t)
                pe.wait_ge(rows_t_ready, t + 1)
                for c in range(DC):
                    last = pe.matmul(in_bank[:, k, :], rows_t[:, k, c, :], w_in_sb[:, c, bass.ds(e, 1), :],
                                     start=(c == 0), stop=(c == DC - 1))
                last.then_inc(hid_filled, 1)

            def step(t, k4, arrivals, more):
                k = k4 % 2
                if more >= 1:
                    widen(t + 1, 1 - k)
                pe.wait_ge(prod_ready, t + 1)
                for c in range(DC):
                    last = pe.transpose(turn_bank[:, k, c * P:(c + 1) * P], prod[:, k, c * P:(c + 1) * P], ident[:, :])
                last.then_inc(turned, 1)
                if more >= 2:
                    turn_rows(t + 2, (k4 + 2) % 4, arrivals)
                e = expert_of(pe, t)
                pe.wait_ge(prod_t_ready, t + 1)
                for c in range(DC):
                    last = pe.matmul(y_bank[:, k, 0:D], prod_t[:, k, c, :], w_out_sb[:, c, bass.ds(e, 1), :],
                                     start=(c == 0), stop=(c == DC - 1))
                last.then_inc(summed, 1)

            turn_rows(0, 0, 16)
            turn_rows(1, 1, 16)
            widen(0, 0)
            with pe.Fori(0, TILES // 4 - 1) as j:
                for k in range(4):
                    step(j * 4 + k, k, (j + 1 + (k >= 2)) * 16, 2)
            last_j = TILES // 4 - 1
            for k in range(4):
                step(last_j * 4 + k, k, (last_j + 1 + (k >= 2)) * 16, min(3 - k, 2))


def combine(nc, h2_dram, y_slots, gates, slots, out):
    with ExitStack() as ctx:
        def sb(name, shape, dt=F32):
            return ctx.enter_context(nc.sbuf_tensor(name, shape, dt))

        def sem(name):
            return ctx.enter_context(nc.semaphore(name))

        RB = 2
        h2 = sb("h2c", [P, RB, NT, D])
        y_k = sb("y_k", [P, RB, K, NT, D])
        gates_now = sb("gates_now", [P, RB, NT, K])
        slot_now = sb("slot_now2", [P, RB, K, NT], mybir.dt.uint32)
        h2_in = [sem("h2_in_0"), sem("h2_in_1")]
        y_in = [sem("y_in_0"), sem("y_in_1")]
        slot_ready = sem("slot_ready")
        passed = sem("passed")
        half_ready = sem("half_ready")
        sum_ready = sem("sum_ready")
        saved = [sem("out_saved_0"), sem("out_saved_1")]
        block = ctx.enter_context(nc.Block())

        @block.sync
        def _(sp):
            def save(b, r):
                sp.wait_ge(sum_ready, b + 1)
                sp.dma_start(out[b, 0:(NT - 1) * P, :].rearrange("(i p) d -> p i d", p=P),
                             h2[:, r, 0:NT - 1, :]).then_inc(saved[r], 16)
                sp.dma_start(out[b, (NT - 1) * P:S, :], h2[0:S - (NT - 1) * P, r, NT - 1, :]).then_inc(saved[r], 16)

            for r in range(RB):
                sp.dma_start(h2[:, r, :, :], h2_dram[r, :, :, :]).then_inc(h2_in[r], 16)
            with sp.Fori(0, B // RB - 1) as j:
                for r in range(RB):
                    save(j * RB + r, r)
                for r in range(RB):
                    sp.wait_ge(saved[r], (j + 1) * 32)
                    sp.dma_start(h2[:, r, :, :], h2_dram[j * RB + RB + r, :, :, :]).then_inc(h2_in[r], 16)
            for r in range(RB):
                save(B - RB + r, r)
            for r in range(RB):
                sp.wait_ge(saved[r], B // RB * 32)

        @block.gpsimd
        def _(pool):
            with pool.Fori(0, B // RB) as j:
                for r in range(RB):
                    pool.wait_ge(slot_ready, j * RB + r + 1)
                    pool.sem_inc(passed, 1)
                    for k in range(K):
                        for i in range(NT):
                            pool.indirect_dma_start(
                                out=y_k[:, r, k, i, :], out_offset=None, in_=y_slots,
                                in_offset=bass.IndirectOffsetOnAxis(ap=slot_now[:, r, k, i:i + 1], axis=0),
                            ).then_inc(y_in[r], 16)

        @block.vector
        def _(dve):
            def indices(b, r):
                dve.tensor_copy(gates_now[:, r, :, :], gates[:, bass.ts(b, NT), :])
                dve.tensor_copy(slot_now[:, r, :, :], slots[:, :, bass.ts(b, NT)]).then_inc(slot_ready, 1)

            def add(b, r, turn):
                dve.wait_ge(slot_ready, b + 1)
                dve.wait_ge(h2_in[r], turn * 16)
                dve.wait_ge(y_in[r], turn * K * NT * 16)
                for k in range(K):
                    for i in range(NT):
                        last = dve.scalar_tensor_tensor(h2[:, r, i, :], y_k[:, r, k, i, :], gates_now[:, r, i, k:k + 1],
                                                        h2[:, r, i, :], ALU.mult, ALU.add)
                    last.then_inc(half_ready if k == 0 else sum_ready, 1)
                    if k == 0:
                        dve.wait_ge(half_ready, b + 1)

            for r in range(RB):
                indices(r, r)
            with dve.Fori(0, B // RB - 1) as j:
                for r in range(RB):
                    add(j * RB + r, r, j + 1)
                    dve.wait_ge(sum_ready, j * RB + r + 1)
                    indices(j * RB + RB + r, r)
            for r in range(RB):
                add(B - RB + r, r, B // RB)


def build(nc, x, wv, bv, wo_t, bo, decay_rev, w_qkv, w_out, router_t, w_in_t, b_in, w_out_t, b_out, out):
    band_dram = nc.dram_tensor("band_dram", (P * 161 + 161,), F32, kind="Internal").ap()
    h2_dram = nc.dram_tensor("h2_dram", (B, P, NT, D), F32, kind="Internal").ap()
    x_slots = nc.dram_tensor("x_slots", (E * REGION, D), F32, kind="Internal").ap()
    y_slots = nc.dram_tensor("y_slots", (TILES * P, D), F32, kind="Internal").ap()
    with (
        nc.sbuf_tensor("gates", [P, B * NT, K], F32) as gates,
        nc.sbuf_tensor("slots", [P, K, B * NT], mybir.dt.uint32) as slots,
        nc.sbuf_tensor("tile_expert", [1, TILES], mybir.dt.int32) as tile_expert,
        nc.sbuf_tensor("tile_row", [1, TILES], mybir.dt.int32) as tile_row,
    ):
        token_mixer_and_attention(nc, x, wv, bv, wo_t, bo, decay_rev, w_qkv, w_out, router_t,
                                  band_dram, h2_dram, x_slots, gates, slots, tile_expert, tile_row)
        experts(nc, w_in_t, b_in, w_out_t, b_out, x_slots, y_slots, tile_expert, tile_row)
        combine(nc, h2_dram, y_slots, gates, slots, out)


def kernel(x, L0_tok_Wv, L0_tok_bv, L0_tok_Wo, L0_tok_bo, L0_tok_decay_w, L0_attn_W_qkv, L0_attn_W_out,
           L0_ffn_router_w, L0_ffn_w_in, L0_ffn_b_in, L0_ffn_w_out, L0_ffn_b_out):
    import numpy as np
    import concourse.bacc as bacc
    from concourse.bass_utils import run_bass_kernel_spmd

    laid_out = {
        "x": x, "wv": L0_tok_Wv, "bv": np.asarray(L0_tok_bv).reshape(DC, P).T, "wo_t": np.asarray(L0_tok_Wo).T, "bo": L0_tok_bo,
        "decay_rev": np.asarray(L0_tok_decay_w)[::-1], "w_qkv": L0_attn_W_qkv, "w_out": L0_attn_W_out,
        "router_t": np.asarray(L0_ffn_router_w).T,
        "w_in_t": np.asarray(L0_ffn_w_in).transpose(2, 0, 1), "b_in": L0_ffn_b_in,
        "w_out_t": np.asarray(L0_ffn_w_out).transpose(2, 0, 1), "b_out": L0_ffn_b_out,
    }
    nc = bacc.Bacc("TRN2", target_bir_lowering=False, num_devices=1)
    arrays, args = {}, []
    for name, a in laid_out.items():
        a = np.ascontiguousarray(a)
        arrays[f"in_{name}"] = a
        args.append(nc.dram_tensor(f"in_{name}", a.shape, mybir.dt.from_np(a.dtype), kind="ExternalInput").ap())
    out = nc.dram_tensor("out", (B, S, D), F32, kind="ExternalOutput").ap()
    build(nc, *args, out)
    r = run_bass_kernel_spmd(nc, [arrays], core_ids=[0])
    return r.results[0]["out"]
```

```python
from contextlib import ExitStack

import concourse.bass as bass
from concourse import mybir

ALU = mybir.AluOpType
ACT = mybir.ActivationFunctionType
AX = mybir.AxisListType
F32 = mybir.dt.float32
F32R = mybir.dt.float32r
BF16 = mybir.dt.bfloat16

P = 128
B, T, D = 8, 750, 256
TAPS = 32
S = T + 1
NT = -(-S // P)
SP_ = NT * P
DC = D // P
H, HD = 16, 16
HC = H // DC
W = 64
NB = SP_ // W
KP = W + SP_
E, I = 8, 256
K = 2
ROWS = B * SP_
REGION = ROWS + P
TILES = ROWS * K // P + E
ROW = D + 2
UNROLL = 8
assert TILES % UNROLL == 0
Y_BUFS = 4
MORE = TILES - ROWS * K // P
BIG = 1e30
EPS = 1e-5
SCALE = float(HD) ** -0.5
HEAD_STEPS, TAIL_STEPS = 16, 14
BANDW = P + TAPS

HALVES = ((0, 4), (4, NT))
ACT_HEAD = ("filtered", "xn_t", "query", "value", "maxima", "scores")
DVE_HEAD = ("h", "key", "max", "out")
MAX_LATE = 4
ACT_ORDER = ([("filtered", k) for k in range(3)] + [("attn_t", k) for k in range(3)]
             + [("xn_t", k) for k in range(3)] + [("query", k) for k in range(3)]
             + [("xn2_t", k) for k in range(3)] + [("value", k) for k in range(3)]
             + [("maxima", 0)] + [("scores", n) for n in range(MAX_LATE)]
             + [("maxima", 1)] + [("scores", n) for n in range(MAX_LATE, 2 * NB)])
RANK_AFTER = 2
BETWEEN_AT = (5, 10, 15, 20, 25, 30, 35, 35, 40, 44)
MAX_FILLS = H // 2
DVE_ORDER = ([("h", k) for k in range(3)] + [("proj", k) for k in range(3)]
             + [("key", k) for k in range(3)] + [("max", n) for n in range(NT * MAX_FILLS)]
             + [("out", i) for i in range(RANK_AFTER)] + [("rank", 0)]
             + [("out", i) for i in range(RANK_AFTER, NT)])
RING = 3
SPLIT_EARLY = 3


def fills_of(order, head, turn):
    heads = [f for f in order if f[0] in head]
    tails = [f for f in order if f[0] not in head]
    if isinstance(turn, int) and turn == 0:
        return heads, 0
    return (tails if isinstance(turn, int) and turn == B else order), (turn - 1) * len(order) + len(heads)


def position(order, head, turn, name, k):
    return fills_of(order, head, turn)[0].index((name, k))


def filled_count(order, head, turn, name, k):
    fills, before = fills_of(order, head, turn)
    return before + (fills.index((name, k)) + 1)


def copied_count(order, head, turn, name, k):
    return filled_count(order, head, turn, name, k) + RING


def free_count(order, head, turn, name, k):
    fills, before = fills_of(order, head, turn)
    return before + max(fills.index((name, k)) + 1, RING)


def token_mixer_and_attention(nc, x, wv, bv, wo_t, bo, decay_rev, w_qkv, w_out, router_t,
                              w_in_t, b_in, w_out_t, b_out, band_dram, sums, x_slots, shared, w_in_loaded, rest_loaded, w_split,
                              tile_expert, tile_row, tile_after):
    with ExitStack() as ctx:
        def sb(name, shape, dt=F32):
            return ctx.enter_context(nc.sbuf_tensor(name, shape, dt))

        def sem(name):
            return ctx.enter_context(nc.semaphore(name))

        act_bank = ctx.enter_context(nc.psum_tensor("act_bank", [P, RING, 512], F32))
        dve_bank = ctx.enter_context(nc.psum_tensor("dve_bank", [P, RING, 512], F32))
        out_bank = ctx.enter_context(nc.psum_tensor("out_bank", [P, 2, 512], F32))

        ident = sb("ident", [P, P])
        ident_b = sb("ident_b", [P, P], BF16)
        band = sb("band", [P, BANDW])
        key_mask = sb("key_mask", [P, 2, 2, P + W], BF16)
        query_mask = sb("query_mask", [W + 3, 2, P], BF16)
        half_neg = sb("half_neg", [P, NT])
        zero = sb("zero", [P, 1])
        decay = sb("decay", [P, TAPS])
        mix_w = sb("mix_w", [P, DC, D])
        bias_h = sb("bias_h", [P, D])
        bv_sb = sb("bv_sb", [P, DC])
        decay_sum = sb("decay_sum", [P, 1])
        bv_sum = sb("bv_sum", [P, DC])
        wqkv_sb = sb("wqkv_sb", [P, DC, 3 * D])
        wout_sb = sb("wout_sb", [P, DC, D])
        rt_sb = sb("rt_sb", [P, DC, E])
        expert_no = sb("expert_no", [P, NT, E])
        before = sb("before", [P, P], BF16)
        ones_b = sb("ones_b", [P, P], BF16)
        row_start = sb("row_start", [P, E])
        region_start = sb("region_start", [P, E])
        tile_no = sb("tile_no", [1, TILES])

        x_sb = shared["x"]
        st = sb("st", [P, DC, SP_])
        h = shared["h"]
        h_kept = sb("h_kept", [P, NT, D])
        attn_rows = sb("attn_rows", [P, NT, D])
        xn2 = sb("xn2", [P, NT, ROW])
        xn2_cols = xn2[:, :, 0:D]
        xn = shared["xn"]
        xnt = sb("xnt", [P, DC, SP_])
        qt = sb("qt", [P, DC, SP_])
        qt_r = sb("qt_r", [P, DC, SP_], F32R)
        kt = sb("kt", [P, DC, KP])
        kt_r = sb("kt_r", [P, DC, KP], F32R)
        q_heads = shared["q_heads"]
        k_heads = shared["k_heads"]
        v_a = shared["v_a"]
        v_b = shared["v_b"]
        qmask_and_max = shared["qmask_and_max"]
        neg_max = sb("neg_max", [P, NT, H])
        max_rest = sb("max_rest", [P, NT, H])
        max_parts = sb("max_parts", [P, NT, 3, H], BF16)
        max_t = sb("max_t", [3 * H, SP_], BF16)
        probs = kt_r[:, :, :].rearrange("p c k -> p (c k)")[:, 0:3 * HC * W].bitcast(F32).rearrange(
            "p (r h q) -> p r h q", r=3, h=HC)
        out_t = sb("out_t", [P, 2, 4, P])
        recip = sb("recip", [P, 2, H])
        wv_sb = xnt[:, :, 0:D]
        bv_wide = xnt[:, :, D:D + P]
        wo_sb = xn[:, 0:DC, :]
        attn = attn_rows[:, :, :].rearrange("p i (h d) -> p i h d", h=H)
        attn_t = xnt[:, :, :]
        h2 = h_kept[:, :, :]
        xn2t = st[:, :, :]
        rest_rows = sb("rest_rows", [P, ROW])
        zeros = x_sb[:, :, :].rearrange("p i d -> p (i d)")[:, 0:161]
        stats = sb("stats", [P, 2, NT, 6])
        moments = sb("moments", [P, 2, NT, 2])
        var_eps = sb("var_eps", [P, 2, NT])
        rstd = sb("rstd", [P, 2, NT])
        logits = sb("logits", [P, NT, E])
        top_logit = sb("top_logit", [P, NT])
        shifted = sb("shifted", [P, NT, E])
        exps = sb("exps", [P, NT, E])
        exp_sum = sb("exp_sum", [P, NT])
        exp_rec = sb("exp_rec", [P, NT])
        rprobs = sb("rprobs", [P, NT, E])
        best = sb("best", [P, NT, 8])
        best_at = sb("best_at", [P, NT, 8], mybir.dt.uint32)
        best_at_f = sb("best_at_f", [P, NT, 8])
        hot0 = sb("hot0", [P, NT, E])
        hot1 = sb("hot1", [P, NT, E])
        chosen = sb("chosen", [P, NT, E], BF16)
        place = sb("place", [P, NT, E])
        place_k = sb("place_k", [P, K, NT, E])
        slot_f = sb("slot_f", [P, K, NT])
        slot_now = sb("slot_now", [P, K, NT], mybir.dt.uint32)
        count = sb("count", [P, E])
        count_i = sb("count_i", [P, E], mybir.dt.int32)
        tiles_of = sb("tiles_of", [P, E])
        first_tile = sb("first_tile", [P, E + 1])
        token_no = sb("token_no", [P, NT])
        jump = sb("jump", [P, E])
        rest_tails = sb("rest_tails", [P, MORE + 1, 2])
        rest_no = sb("rest_no", [P, MORE + 1])
        reached = attn_rows[:, :, :].rearrange("p i d -> p (i d)")[0:1, 0:TILES * E].rearrange("p (t e) -> p t e", e=E)
        jumped = xnt[:, :, :].rearrange("p c s -> p (c s)")[0:1, 0:TILES * E].rearrange("p (t e) -> p t e", e=E)
        wait_for = sb("wait_for", [1, TILES])
        wait_parts = st[:, :, :].rearrange("p c s -> p (c s)")[0:1, 0:TILES * E].rearrange("p (t e) -> p t e", e=E)
        reach_sum = sb("reach_sum", [1, TILES])
        jump_sum = sb("jump_sum", [1, TILES])
        tile_start = sb("tile_start", [1, TILES])
        end_row = sb("end_row", [1, E], mybir.dt.int32)

        weights_in = sem("weights_in")
        w_high_ready = sem("w_high_ready")
        small_in = sem("small_in")
        decay_in = sem("decay_in")
        rest_in = sem("rest_in")
        tail_zeroed = sem("tail_zeroed")
        row_start_ready = sem("row_start_ready")
        band_zeroed = sem("band_zeroed")
        band_written = sem("band_written")
        band_in = sem("band_in")
        consts_ready = sem("consts_ready")
        zeros_ready = sem("zeros_ready")
        zero_ready = sem("zero_ready")
        max_consts = sem("max_consts")
        heads_zeroed = sem("heads_zeroed")
        pool_chain = sem("pool_chain")
        dve_passed = sem("dve_passed")
        pe_passed = sem("pe_passed")
        pool_passed = sem("pool_passed")
        sp_passed = sem("sp_passed")
        setup_chain = sem("setup_chain")
        setup_mm = sem("setup_mm")
        mix_ready = sem("mix_ready")
        x_in = sem("x_in")
        conv_done = sem("conv_done")
        act_filled = sem("act_filled")
        act_copied = sem("act_copied")
        dve_filled = sem("dve_filled")
        dve_copied = sem("dve_copied")
        out_copied = sem("out_copied")
        xn_ready = [sem("xn_ready"), sem("xn2_ready")]
        head_chain = sem("head_chain")
        tail_chain = sem("tail_chain")
        var_ready = [sem("var_ready"), sem("var2_ready")]
        rstd_ready = [sem("rstd_ready"), sem("rstd2_ready")]
        h_copied = sem("h_copied")
        ident_ready = sem("ident_ready")
        k_rounded = sem("k_rounded")
        q_placed = sem("q_placed")
        k_placed = sem("k_placed")
        v_shifted = sem("v_shifted")
        parts_ready = sem("parts_ready")
        max_placed = [sem("max_placed_0"), sem("max_placed_1")]
        maxes_done = sem("maxes_done")
        probs_used = sem("probs_used")
        h2_saved = sem("h2_saved")
        chosen_ready = sem("chosen_ready")
        slots_ready = sem("slots_ready")
        scattered = [sem("scattered_0"), sem("scattered_1")]
        second_gates = sem("second_gates")
        ends_ready = sem("ends_ready")
        ends_cleared = sem("ends_cleared")
        rest_zeroed = sem("rest_zeroed")
        rest_numbered = sem("rest_numbered")
        shifted_ready = sem("shifted_ready")
        exps_ready = sem("exps_ready")
        routed = sem("routed")
        logits_copied = sem("logits_copied")

        def act_free(turn, name, k):
            return free_count(ACT_ORDER, ACT_HEAD, turn, name, k)

        def act_has(turn, name, k):
            return copied_count(ACT_ORDER, ACT_HEAD, turn, name, k)

        def dve_free(turn, name, k):
            return free_count(DVE_ORDER, DVE_HEAD, turn, name, k)

        def dve_has(turn, name, k):
            return copied_count(DVE_ORDER, DVE_HEAD, turn, name, k)

        def act_slot(turn, name, k):
            return act_bank[:, position(ACT_ORDER, ACT_HEAD, turn, name, k) % RING, :]

        def dve_slot(turn, name, k):
            return dve_bank[:, position(DVE_ORDER, DVE_HEAD, turn, name, k) % RING, :]

        def parts_of(turn):
            return not (isinstance(turn, int) and turn == B), not (isinstance(turn, int) and turn == 0)

        def probs_before(b):
            return b * 2 * NB + 3

        N_PLACE = HC * 16
        N_CONSTS = 12
        N_SCATTER = NT * 16

        def thirds(dst, bank, off=0):
            return [(dst[:, 0, off:off + 512], bank[:, 0:512]),
                    (dst[:, 1, off:off + 512], bank[:, 0:512]),
                    (dst[:, 0:2, off + 512:off + SP_], bank[:, 0:512].rearrange("p (c n) -> p c n", c=2))]

        block = ctx.enter_context(nc.Block())

        @block.sync
        def _(sp):
            sp.dma_start(decay[:, :], decay_rev.partition_broadcast(P)).then_inc(decay_in, 16)
            sp.wait_ge(zeros_ready, 1)
            sp.dma_start(band_dram[0:P * 161].rearrange("(p j) -> p j", j=161), zeros).then_inc(band_zeroed, 16)
            sp.wait_ge(band_zeroed, 16)
            sp.wait_ge(decay_in, 16)
            sp.dma_start(band_dram[1:1 + P * 161].rearrange("(p j) -> p j", j=161)[:, 0:TAPS],
                         decay[:, :]).then_inc(band_written, 16)
            sp.wait_ge(band_written, 16)
            sp.dma_start(band[:, :], band_dram[0:P * BANDW].rearrange("(p j) -> p j", j=BANDW)).then_inc(band_in, 16)

            def turn(t):
                has_head, has_tail = parts_of(t)
                if has_tail:
                    sp.wait_ge(dve_copied, dve_has(t, "proj", 2))
                    sp.dma_start(sums[bass.ds((t - 1) * SP_, SP_), :].rearrange("(i p) d -> p i d", p=P),
                                 h2[:, :, :]).then_inc(h2_saved, 16)
                if not has_head:
                    return
                if not has_tail:
                    sp.wait_ge(heads_zeroed, 5)
                sp.wait_ge(k_rounded, t * 3 + 3)
                for g in range(HC):
                    sp.dma_start(k_heads[g * HD:(g + 1) * HD, :, g % (HC // 2), :].bitcast(F32),
                                 kt_r[g * HD:(g + 1) * HD, :, :].bitcast(F32)).then_inc(k_placed, 16)
                sp.wait_ge(act_copied, act_has(t, "query", 2))
                sp.wait_ge(probs_used, probs_before(t))
                for g in range(HC):
                    sp.dma_start(q_heads[g * HD:(g + 1) * HD, :, g % (HC // 2), :],
                                 qt[g * HD:(g + 1) * HD, :, :]).then_inc(q_placed, 16)
                sp.wait_ge(act_copied, act_has(t, "value", 2))
                sp.dma_start(v_b[W:P, :, :, :], v_a[0:W, :, :, :]).then_inc(v_shifted, 16)
                sp.dma_start(v_b[0:W, 1:NT, :, :], v_a[W:P, 0:NT - 1, :, :]).then_inc(v_shifted, 16)
                for half, (i0, i1) in enumerate(HALVES):
                    sp.wait_ge(act_copied, act_has(t, "maxima", half))
                    for k in range(3):
                        sp.dma_start(qmask_and_max[W + k:W + k + 1, :, i0 * P:i1 * P],
                                     max_t[k * H:(k + 1) * H, i0 * P:i1 * P]).then_inc(max_placed[half], 16)
                sp.wait_ge(maxes_done, t + 1)
                sp.sem_inc(sp_passed, 1)

            turn(0)
            with sp.Fori(1, B) as t:
                turn(t)
            sp.wait_ge(probs_used, probs_before(B))
            sp.wait_ge(scattered[1], (B - 1) * N_SCATTER)
            sp.dma_start(shared["w_in"], w_in_t.rearrange("(c p) e n -> p c e n", p=P)).then_inc(w_in_loaded, 16)
            turn(B)
            sp.wait_ge(rest_numbered, 2)
            past = x_slots[E * REGION:E * REGION + MORE * P, :].rearrange("(s p) d -> p s d", p=P)
            sp.dma_start(past[:, :, 0:D],
                         rest_rows[:, 0:D].unsqueeze(1).to_broadcast([P, MORE, D])).then_inc(ends_cleared, 16)
            sp.dma_start(past[:, :, D:ROW], rest_tails[:, 1:, :]).then_inc(ends_cleared, 16)
            sp.dma_start(sums[ROWS:ROWS + (MORE + 1) * P, :].rearrange("(s p) d -> p s d", p=P),
                         rest_rows[:, 0:D].unsqueeze(1).to_broadcast([P, MORE + 1, D])).then_inc(ends_cleared, 16)
            sp.wait_ge(ends_ready, 1)
            for e in range(E):
                at = sp.value_load(end_row[0:1, e:e + 1], min_val=e * REGION, max_val=e * REGION + ROWS)
                sp.dma_start(x_slots[bass.ds(at, P), :], rest_rows[:, :]).then_inc(ends_cleared, 16)
            sp.wait_ge(ends_cleared, (E + 3) * 16)
            sp.wait_ge(h2_saved, B * 16)

        @block.gpsimd
        def _(pool):
            pool.memset(zeros, 0.0).then_inc(zeros_ready, 1)
            pool.dma_start(bv_sb[:, :], bv).then_inc(small_in, 16)
            pool.dma_start(bias_h[:, :], bo.partition_broadcast(P)).then_inc(small_in, 16)
            pool.memset(ident[:, :], 1.0).then_inc(pool_chain, 1)
            pool.memset(zero[:, :], 0.0).then_inc(zero_ready, 1)
            pool.memset(half_neg[:, :], -0.5).then_inc(pool_chain, 1)
            pool.wait_ge(pool_chain, 2)
            pool.affine_select(ident[:, :], ident[:, :], [[-1, P]], ALU.is_equal, 0.0, base=0,
                               channel_multiplier=1).then_inc(ident_ready, 1)
            pool.wait_ge(band_zeroed, 16)

            def load_x(b):
                pool.dma_start(x_sb[:, 0:NT - 1, :],
                               x[b, 0:(NT - 1) * P, :].rearrange("(i p) d -> p i d", p=P)).then_inc(x_in, 16)
                pool.dma_start(x_sb[0:T - (NT - 1) * P, NT - 1, :], x[b, (NT - 1) * P:T, :]).then_inc(x_in, 16)

            pool.wait_ge(tail_zeroed, 1)
            load_x(0)
            pool.memset(ident_b[:, :], 1.0).then_inc(pool_chain, 1)
            pool.memset(key_mask[:, :, :, :], 0.0).then_inc(pool_chain, 1)
            pool.wait_ge(pool_chain, 4)
            pool.affine_select(ident_b[:, :], ident_b[:, :], [[-1, P]], ALU.is_equal, 0.0, base=0,
                               channel_multiplier=1).then_inc(max_consts, 1)
            km = key_mask[:, :, :, :].rearrange("p a b k -> p (a b) k")
            pool.affine_select(km, km, [[0, 4], [1, P + W]], ALU.is_gt, -BIG, base=0,
                               channel_multiplier=-1).then_inc(pool_chain, 1)
            pool.wait_ge(pool_chain, 5)
            pool.affine_select(km, km, [[0, 4], [-1, P + W]], ALU.is_ge, -BIG, base=W,
                               channel_multiplier=1).then_inc(pool_chain, 1)
            pool.wait_ge(pool_chain, 6)
            km0 = key_mask[:, 0, :, :]
            pool.affine_select(km0, km0, [[0, 2], [1, P + W]], ALU.is_ge, -BIG, base=-W,
                               channel_multiplier=0).then_inc(max_consts, 1)

            def masks_late():
                pool.memset(qmask_and_max[0:W, :, :], 1.0).then_inc(pool_chain, 1)
                pool.memset(query_mask[0:W, :, :], 0.0).then_inc(pool_chain, 1)
                pool.memset(ones_b[:, :], 1.0).then_inc(pool_chain, 1)
                pool.wait_ge(pool_chain, 9)
                im = qmask_and_max[0:W, :, :].rearrange("p h (n w) -> p (h n) w", w=W)
                pool.affine_select(im, im, [[0, H * NB], [-1, W]], ALU.is_equal, 0.0, base=0,
                                   channel_multiplier=1).then_inc(consts_ready, 1)
                qm = query_mask[0:W, :, :]
                pool.affine_select(qm, qm, [[0, 2], [1, P]], ALU.is_gt, -BIG, base=0,
                                   channel_multiplier=-1).then_inc(pool_chain, 1)
                pool.wait_ge(pool_chain, 10)
                pool.affine_select(qm, qm, [[0, 2], [-1, P]], ALU.is_ge, -BIG, base=W,
                                   channel_multiplier=1).then_inc(pool_chain, 1)
                pool.wait_ge(pool_chain, 11)
                qm0 = query_mask[0:W, 0, :]
                pool.affine_select(qm0, qm0, [[1, P]], ALU.is_ge, -BIG, base=-W,
                                   channel_multiplier=0).then_inc(consts_ready, 1)
                pool.iota(tile_no[:, :], [[1, TILES]], base=0, channel_multiplier=0,
                          allow_small_or_imprecise_dtypes=True).then_inc(consts_ready, 1)
                pool.iota(region_start[:, :], [[REGION, E]], base=0, channel_multiplier=0,
                          allow_small_or_imprecise_dtypes=True).then_inc(consts_ready, 1)
                pool.affine_select(before[:, :], ones_b[:, :], [[1, P]], ALU.is_gt, 0.0, base=0,
                                   channel_multiplier=-1).then_inc(consts_ready, 1)
                pool.iota(expert_no[:, :, :], [[0, NT], [1, E]], base=0, channel_multiplier=0,
                          allow_small_or_imprecise_dtypes=True).then_inc(consts_ready, 1)
                pool.iota(token_no[:, :], [[P, NT]], base=0, channel_multiplier=1,
                          allow_small_or_imprecise_dtypes=True).then_inc(consts_ready, 1)
                pool.iota(rest_no[:, :], [[P, MORE + 1]], base=ROWS, channel_multiplier=1,
                          allow_small_or_imprecise_dtypes=True).then_inc(consts_ready, 1)

            def turn(t, more):
                has_head, has_tail = parts_of(t)
                if has_head:
                    pool.wait_ge(var_ready[0], t + 1)
                    pool.tensor_tensor(rstd[:, 0, :], var_eps[:, 0, :], half_neg[:, :], ALU.pow).then_inc(rstd_ready[0], 1)
                    if more:
                        pool.wait_ge(conv_done, t + 1)
                        load_x(t + 1)
                    if not has_tail:
                        masks_late()
                if has_tail:
                    pool.wait_ge(var_ready[1], t)
                    pool.tensor_tensor(rstd[:, 1, :], var_eps[:, 1, :], half_neg[:, :], ALU.pow).then_inc(rstd_ready[1], 1)
                if has_head:
                    if has_tail:
                        pool.wait_ge(xn_ready[1], t * NT)
                        pool.wait_ge(h2_saved, t * 16)
                        pool.sem_inc(pool_passed, 1)
                    pool.tensor_copy(h_kept[:, :, :], h[:, :, :]).then_inc(h_copied, 1)
                    if not more:
                        pool.wait_ge(h_copied, B)
                        pool.wait_ge(maxes_done, B)
                        pool.dma_start(shared["b_in"], b_in.rearrange("e n -> (e n)").partition_broadcast(P)).then_inc(rest_loaded, 16)
                        pool.dma_start(shared["b_out"], b_out.rearrange("e n -> (e n)").partition_broadcast(P)).then_inc(rest_loaded, 16)
                        pool.dma_start(shared["w_out"], w_out_t.rearrange("(c p) e n -> p c e n", p=P)).then_inc(rest_loaded, 16)
                if has_tail:
                    pool.wait_ge(slots_ready, t)
                    pool.sem_inc(pool_passed, 1)
                    for k in range(K):
                        if k == 1:
                            pool.wait_ge(scattered[0], t * N_SCATTER)
                            pool.sem_inc(pool_passed, 1)
                            pool.tensor_copy(xn2[:, :, D], best[:, :, 1]).then_inc(second_gates, 1)
                            pool.wait_ge(second_gates, t)
                            pool.sem_inc(pool_passed, 1)
                        for i in range(NT):
                            pool.indirect_dma_start(
                                out=x_slots, out_offset=bass.IndirectOffsetOnAxis(ap=slot_now[:, k, i:i + 1], axis=0),
                                in_=xn2[:, i, :], in_offset=None).then_inc(scattered[k], 16)

            turn(0, True)
            with pool.Fori(1, B - 1) as t:
                turn(t, True)
            turn(B - 1, False)
            turn(B, False)
            for k in range(K):
                pool.wait_ge(scattered[k], B * N_SCATTER)

        @block.scalar
        def _(act):
            act.dma_start(wv_sb[:, :, :], wv.rearrange("(c p) n -> p c n", p=P)).then_inc(weights_in, 16)
            act.dma_start(wo_sb[:, :, :], wo_t.rearrange("(c p) n -> p c n", p=P)).then_inc(weights_in, 16)
            act.dma_start(wqkv_sb[:, :, :], w_qkv.rearrange("(c p) n -> p c n", p=P)).then_inc(rest_in, 16)
            act.dma_start(wout_sb[:, :, :], w_out.rearrange("(c p) n -> p c n", p=P)).then_inc(rest_in, 16)
            act.dma_start(rt_sb[:, :, :], router_t.rearrange("(c p) n -> p c n", p=P)).then_inc(rest_in, 16)
            act.wait_ge(setup_mm, 1)
            act.copy(mix_w[:, :, :], act_bank[:, 0, :].rearrange("p (c n) -> p c n", c=DC)).then_inc(mix_ready, 1)
            act.wait_ge(mix_ready, 1)
            act.wait_ge(zero_ready, 1)
            act.sem_inc(act_copied, RING)

            def split_high(e0, e1):
                act.wait_ge(w_in_loaded, 16)
                for e in range(e0, e1):
                    act.copy(shared["w_high"][:, :, e, :], shared["w_in"][:, :, e, :]).then_inc(w_high_ready, 1)

            def turn(t):
                has_head, has_tail = parts_of(t)

                def fill(name, k):
                    act.wait_ge(act_filled, filled_count(ACT_ORDER, ACT_HEAD, t, name, k))
                    return act_slot(t, name, k)

                def copy_thirds(name, dst):
                    for k in range(3):
                        bank = fill(name, k)
                        d, s = thirds(dst, bank)[k]
                        act.copy(d, s).then_inc(act_copied, 1)

                def probabilities(n):
                    bank = fill("scores", n)
                    act.wait_ge(probs_used, t * 2 * NB + n + 1)
                    act.activation(probs[:, n % 3, :, :], bank.rearrange("p (h q) -> p h q", h=HC),
                                   ACT.Exp).then_inc(act_copied, 1)

                def maxima(half):
                    i0, i1 = HALVES[half]
                    bank = fill("maxima", half)
                    act.copy(max_t[:, i0 * P:i1 * P],
                             bank.bitcast(BF16)[0:3 * H, 0:(i1 - i0) * P]).then_inc(act_copied, 1)

                if has_head:
                    copy_thirds("filtered", st)
                if not has_tail:
                    for c in range(DC):
                        act.copy(q_heads[:, c, :, :].rearrange("p a s -> p (a s)"),
                                 zero[:, 0:1].to_broadcast([P, HC // 2 * SP_])).then_inc(heads_zeroed, 1)
                if has_tail:
                    copy_thirds("attn_t", attn_t)
                if has_head:
                    copy_thirds("xn_t", xnt)
                    for k in range(3):
                        act.wait_ge(dve_copied, dve_has(t, "key", k))
                        d = (kt_r[:, 0, W:W + 512], kt_r[:, 1, W:W + 512], kt_r[:, :, W + 512:KP])[k]
                        s = (kt[:, 0, W:W + 512], kt[:, 1, W:W + 512], kt[:, :, W + 512:KP])[k]
                        act.copy(d, s).then_inc(k_rounded, 1)
                    for k in range(3):
                        bank = fill("query", k)
                        d, s = thirds(qt, bank)[k]
                        act.mul(d, s, SCALE)
                        d, s = thirds(qt_r, bank)[k]
                        act.mul(d, s, SCALE).then_inc(act_copied, 1)
                if has_tail:
                    copy_thirds("xn2_t", xn2t)

                def exponentials():
                    act.wait_ge(shifted_ready, t)
                    act.activation(exps[:, :, :], shifted[:, :, :], ACT.Exp).then_inc(exps_ready, 1)

                if not has_head:
                    split_high(0, SPLIT_EARLY)
                    exponentials()
                    split_high(SPLIT_EARLY, E)
                    return
                for k in range(3):
                    bank = fill("value", k)
                    act.copy(v_a[:, 2 * k:2 * k + 2, :, 0:HD],
                             bank.rearrange("p (i h d) -> p i h d", i=2, h=H)).then_inc(act_copied, 1)
                maxima(0)
                for n in range(MAX_LATE):
                    probabilities(n)
                maxima(1)
                if has_tail:
                    exponentials()
                for n in range(MAX_LATE, 2 * NB):
                    probabilities(n)
                act.wait_ge(q_placed, (t + 1) * N_PLACE)
                act.wait_ge(k_placed, (t + 1) * N_PLACE)
                act.wait_ge(v_shifted, (t + 1) * 32)
                for half in range(2):
                    act.wait_ge(max_placed[half], (t + 1) * 48)

            turn(0)
            with act.Fori(1, B) as t:
                turn(t)
            turn(B)

        @block.vector
        def _(dve):
            dve.memset(x_sb[96:P, NT - 1, :], 0.0).then_inc(tail_zeroed, 1)
            dve.wait_ge(small_in, 32)
            dve.wait_ge(decay_in, 16)
            dve.tensor_reduce(decay_sum[:, :], decay[:, :], AX.X, ALU.add).then_inc(setup_chain, 1)
            dve.wait_ge(setup_chain, 1)
            dve.tensor_scalar(bv_sum[:, :], bv_sb[:, :], decay_sum[:, 0:1], None, ALU.mult).then_inc(setup_chain, 1)
            dve.wait_ge(setup_chain, 2)
            dve.tensor_copy(bv_wide[:, :, :], bv_sum[:, :].unsqueeze(2).to_broadcast([P, DC, P])).then_inc(setup_chain, 1)
            dve.memset(query_mask[W:W + 3, :, :], 1.0).then_inc(consts_ready, 1)
            dve.memset(v_b[0:W, 0, :, :], 0.0).then_inc(consts_ready, 1)
            dve.memset(kt[:, :, 0:W], 0.0).then_inc(consts_ready, 1)
            dve.memset(kt_r[:, :, 0:W].bitcast(F32), 0.0).then_inc(heads_zeroed, 1)
            dve.wait_ge(setup_mm, 2)
            dve.tensor_tensor(bias_h[:, :], dve_bank[:, 0, 0:D], bias_h[:, :], ALU.add).then_inc(dve_copied, RING)
            dve.sem_inc(out_copied, 2)
            dve.memset(k_heads[:, 0, :, :].bitcast(F32), 0.0).then_inc(heads_zeroed, 1)
            dve.wait_ge(dve_copied, RING)

            def split_low(e0, e1):
                for e in range(e0, e1):
                    dve.wait_ge(w_high_ready, e + 1)
                    dve.tensor_tensor(shared["w_low"][:, :, e, :], shared["w_in"][:, :, e, :],
                                      shared["w_high"][:, :, e, :], ALU.subtract).then_inc(w_split, 1)

            def turn(t):
                has_head, has_tail = parts_of(t)
                steps = {"head": 0, "tail": 0}

                def head_step(ins):
                    steps["head"] += 1
                    ins.then_inc(head_chain, 1)
                    dve.wait_ge(head_chain, t * HEAD_STEPS + steps["head"])

                def tail_step(ins):
                    steps["tail"] += 1
                    ins.then_inc(tail_chain, 1)
                    dve.wait_ge(tail_chain, (t - 1) * TAIL_STEPS + steps["tail"])

                def fill(name, k):
                    dve.wait_ge(dve_filled, filled_count(DVE_ORDER, DVE_HEAD, t, name, k))
                    return dve_slot(t, name, k)

                def norm_moments(src, norm, step):
                    for i in range(NT):
                        last = dve.bn_stats(stats[:, norm, i, :], src[:, i, :])
                    step(last)
                    dve.sem_inc(dve_passed, 1)
                    for i in range(NT):
                        last = dve.bn_aggr(moments[:, norm, i, :], stats[:, norm, i, :])
                    step(last)
                    dve.tensor_scalar(var_eps[:, norm, :], moments[:, norm, :, 1], EPS, None,
                                      ALU.add).then_inc(var_ready[norm], 1)

                def norm_rows(src, dst, norm, batch):
                    dve.wait_ge(rstd_ready[norm], batch + 1)
                    for i in range(NT):
                        dve.tensor_scalar(dst[:, i, :], src[:, i, :], moments[:, norm, i, 0:1],
                                          rstd[:, norm, i:i + 1], ALU.subtract, ALU.mult).then_inc(xn_ready[norm], 1)

                def split_maxima(half):
                    tiles = slice(*HALVES[half])
                    head_step(dve.tensor_copy(max_parts[:, tiles, 0, :], neg_max[:, tiles, :]))
                    head_step(dve.tensor_tensor(max_rest[:, tiles, :], neg_max[:, tiles, :],
                                                max_parts[:, tiles, 0, :], ALU.subtract))
                    head_step(dve.tensor_copy(max_parts[:, tiles, 1, :], max_rest[:, tiles, :]))
                    head_step(dve.tensor_tensor(max_rest[:, tiles, :], max_rest[:, tiles, :],
                                                max_parts[:, tiles, 1, :], ALU.subtract))
                    dve.tensor_copy(max_parts[:, tiles, 2, :], max_rest[:, tiles, :]).then_inc(parts_ready, 1)

                def shift_logits():
                    dve.wait_ge(routed, t)
                    dve.tensor_copy(logits[:, :, :], out_bank[:, 1, 0:NT * E].rearrange("p (i e) -> p i e", e=E)
                                    ).then_inc(logits_copied, 1)
                    dve.wait_ge(logits_copied, t)
                    tail_step(dve.tensor_reduce(top_logit[:, :], logits[:, :, :], AX.X, ALU.max))
                    dve.tensor_tensor(shifted[:, :, :], logits[:, :, :],
                                      top_logit[:, :].unsqueeze(2).to_broadcast([P, NT, E]),
                                      ALU.subtract).then_inc(shifted_ready, 1)

                def choose_experts():
                    dve.wait_ge(exps_ready, t)
                    tail_step(dve.tensor_reduce(exp_sum[:, :], exps[:, :, :], AX.X, ALU.add))
                    tail_step(dve.reciprocal(exp_rec[:, :], exp_sum[:, :]))
                    tail_step(dve.tensor_tensor(rprobs[:, :, :], exps[:, :, :],
                                                exp_rec[:, :].unsqueeze(2).to_broadcast([P, NT, E]), ALU.mult))
                    dve.sem_inc(dve_passed, 1)
                    for i in range(NT):
                        last = dve.max(best[:, i, :], rprobs[:, i, :])
                    tail_step(last)
                    dve.sem_inc(dve_passed, 1)
                    for i in range(NT):
                        last = dve.max_index(best_at[:, i, :], best[:, i, :], rprobs[:, i, :])
                    tail_step(last)
                    tail_step(dve.tensor_copy(best_at_f[:, :, :], best_at[:, :, :]))
                    dve.tensor_tensor(hot0[:, :, :], expert_no[:, :, :],
                                      best_at_f[:, :, 0:1].to_broadcast([P, NT, E]), ALU.is_equal)
                    tail_step(dve.tensor_tensor(hot1[:, :, :], expert_no[:, :, :],
                                                best_at_f[:, :, 1:2].to_broadcast([P, NT, E]), ALU.is_equal))
                    dve.tensor_tensor(chosen[:, :, :], hot0[:, :, :], hot1[:, :, :], ALU.add).then_inc(chosen_ready, 1)
                    dve.tensor_copy(xn2[:, :, D], best[:, :, 0])
                    tail_step(dve.tensor_copy(xn2[:, :, D + 1].bitcast(mybir.dt.uint32), token_no[:, :]))
                    dve.tensor_scalar(token_no[:, :], token_no[:, :], float(SP_), None, ALU.add)

                def give_slots():
                    bank = fill("rank", 0)
                    rank = bank[:, 0:NT * E].rearrange("p (i e) -> p i e", e=E)
                    tail_step(dve.tensor_tensor(place[:, :, :], rank,
                                                row_start[:, :].unsqueeze(1).to_broadcast([P, NT, E]), ALU.add))
                    dve.tensor_tensor(row_start[:, :], row_start[:, :], bank[:, NT * E:NT * E + E],
                                      ALU.add).then_inc(dve_copied, 1)
                    dve.tensor_tensor(place_k[:, 0, :, :], place[:, :, :], hot0[:, :, :], ALU.mult)
                    tail_step(dve.tensor_tensor(place_k[:, 1, :, :], place[:, :, :], hot1[:, :, :], ALU.mult))
                    tail_step(dve.tensor_reduce(slot_f[:, :, :], place_k[:, :, :, :], AX.X, ALU.add))
                    dve.tensor_copy(slot_now[:, :, :], slot_f[:, :, :]).then_inc(slots_ready, 1)

                if has_head:
                    for k in range(3):
                        bank = fill("h", k)
                        dve.tensor_tensor(h[:, 2 * k:2 * k + 2, :], bank.rearrange("p (i d) -> p i d", i=2),
                                          bias_h[:, :].unsqueeze(1).to_broadcast([P, 2, D]), ALU.add).then_inc(dve_copied, 1)
                    dve.wait_ge(dve_copied, dve_has(t, "h", 2))
                    norm_moments(h, 0, head_step)
                    norm_rows(h, xn, 0, t)
                if not has_tail:
                    dve.memset(k_heads[:, 1, :, :].bitcast(F32), 0.0).then_inc(heads_zeroed, 1)
                    dve.memset(v_a[:, :, :, HD:2 * HD], 1.0).then_inc(consts_ready, 1)
                if has_tail:
                    for k in range(3):
                        bank = fill("proj", k)
                        dve.tensor_tensor(h2[:, 2 * k:2 * k + 2, :], bank.rearrange("p (i d) -> p i d", i=2),
                                          h_kept[:, 2 * k:2 * k + 2, :], ALU.add).then_inc(dve_copied, 1)
                    dve.wait_ge(dve_copied, dve_has(t, "proj", 2))
                    norm_moments(h2, 1, tail_step)
                if has_head:
                    for k in range(3):
                        bank = fill("key", k)
                        d, s = thirds(kt, bank, W)[k]
                        dve.tensor_copy(d, s).then_inc(dve_copied, 1)
                if has_tail:
                    norm_rows(h2, xn2_cols, 1, t - 1)
                if not has_head:
                    split_low(0, SPLIT_EARLY)
                    shift_logits()
                    choose_experts()
                    give_slots()
                    assert steps["tail"] == TAIL_STEPS
                    return
                for half, (i0, i1) in enumerate(HALVES):
                    for n in range(i0 * MAX_FILLS, i1 * MAX_FILLS):
                        i, g = divmod(n, MAX_FILLS)
                        bank = fill("max", n)
                        dve.tensor_reduce(neg_max[:, i, 2 * g:2 * g + 2],
                                          bank[:, 0:2 * (P + W)].rearrange("p (h k) -> p h k", h=2),
                                          AX.X, ALU.max, negate=True).then_inc(dve_copied, 1)
                    dve.wait_ge(dve_copied, dve_has(t, "max", i1 * MAX_FILLS - 1))
                    split_maxima(half)
                if has_tail:
                    shift_logits()
                for i in range(NT + 1):
                    if i < NT:
                        dve.wait_ge(probs_used, probs_before(t) + 4 * (i + 1))
                        dve.tensor_copy(out_t[:, i % 2, :, :],
                                        out_bank[:, i % 2, :].rearrange("p (g q) -> p g q", g=4)).then_inc(out_copied, 1)
                    if has_tail and i == 0:
                        choose_experts()
                    if i >= 1:
                        j = i - 1
                        back = fill("out", j).rearrange("p (h d) -> p h d", d=2 * HD)
                        head_step(dve.reciprocal(recip[:, j % 2, :], back[:, :, HD]))
                        dve.tensor_tensor(attn[:, j, :, :], back[:, :, 0:HD],
                                          recip[:, j % 2, :].unsqueeze(2).to_broadcast([P, H, HD]),
                                          ALU.mult).then_inc(dve_copied, 1)
                        if has_tail and j == RANK_AFTER - 1:
                            give_slots()
                dve.wait_ge(h_copied, t + 1)
                dve.wait_ge(k_rounded, t * 3 + 3)
                if has_tail:
                    for k in range(K):
                        dve.wait_ge(scattered[k], t * N_SCATTER)
                assert steps["head"] == HEAD_STEPS and steps["tail"] in (0, TAIL_STEPS), steps

            turn(0)
            dve.wait_ge(consts_ready, N_CONSTS)
            dve.tensor_copy(row_start[:, :], region_start[:, :]).then_inc(row_start_ready, 1)
            dve.wait_ge(row_start_ready, 1)
            with dve.Fori(1, B) as t:
                turn(t)
            dve.memset(rest_rows[:, :], 0.0).then_inc(rest_zeroed, 1)
            dve.memset(rest_tails[:, :, :], 0.0).then_inc(rest_zeroed, 1)
            dve.wait_ge(rest_zeroed, 2)
            dve.tensor_copy(rest_rows[:, D + 1:D + 2].bitcast(mybir.dt.uint32), rest_no[:, 0:1]).then_inc(rest_numbered, 1)
            dve.tensor_copy(rest_tails[:, :, 1].bitcast(mybir.dt.uint32), rest_no[:, :]).then_inc(rest_numbered, 1)
            turn(B)

            end_chain = [0]

            def last_(ins):
                end_chain[0] += 1
                ins.then_inc(setup_chain, 1)
                dve.wait_ge(setup_chain, 3 + end_chain[0])

            dve.wait_ge(dve_copied, dve_has(B, "rank", 0))
            dve.tensor_copy(end_row[:, :], row_start[0:1, :]).then_inc(ends_ready, 1)
            last_(dve.tensor_tensor(count[:, :], row_start[:, :], region_start[:, :], ALU.subtract))
            last_(dve.tensor_scalar(count[:, :], count[:, :], float(P - 1), None, ALU.add))
            last_(dve.tensor_copy(count_i[:, :], count[:, :]))
            last_(dve.tensor_scalar(count_i[:, :], count_i[:, :], P.bit_length() - 1, None, ALU.arith_shift_right))
            last_(dve.tensor_copy(tiles_of[:, :], count_i[:, :]))
            last_(dve.memset(first_tile[:, 0:1], 0.0))
            for e in range(E):
                last_(dve.tensor_tensor(first_tile[:, e + 1:e + 2], first_tile[:, e:e + 1], tiles_of[:, e:e + 1], ALU.add))
            last_(dve.tensor_scalar(jump[:, :], tiles_of[:, :], -float(P), float(REGION), ALU.mult, ALU.add))
            last_(dve.tensor_tensor(reached[:, :, :], tile_no[:, :].unsqueeze(2).to_broadcast([1, TILES, E]),
                                    first_tile[0:1, 1:E + 1].unsqueeze(1).to_broadcast([1, TILES, E]), ALU.is_ge))
            last_(dve.tensor_tensor(jumped[:, :, :], reached[:, :, :],
                                    jump[0:1, :].unsqueeze(1).to_broadcast([1, TILES, E]), ALU.mult))
            last_(dve.tensor_tensor(wait_parts[:, :, :], reached[:, :, :],
                                    tiles_of[0:1, :].unsqueeze(1).to_broadcast([1, TILES, E]), ALU.mult))
            last_(dve.tensor_reduce(wait_for[:, :], wait_parts[:, :, :], AX.X, ALU.add))
            last_(dve.tensor_scalar(wait_for[:, :], wait_for[:, :], 1.0, None, ALU.add))
            last_(dve.tensor_copy(tile_after[:, :], wait_for[:, :]))
            last_(dve.tensor_reduce(reach_sum[:, :], reached[:, :, :], AX.X, ALU.add))
            last_(dve.tensor_reduce(jump_sum[:, :], jumped[:, :, :], AX.X, ALU.add))
            last_(dve.tensor_scalar(reach_sum[:, :], reach_sum[:, :], float(E - 1), None, ALU.min))
            last_(dve.tensor_scalar(tile_start[:, :], tile_no[:, :], float(P), None, ALU.mult))
            last_(dve.tensor_tensor(jump_sum[:, :], jump_sum[:, :], tile_start[:, :], ALU.add))
            dve.tensor_copy(tile_expert[:, :], reach_sum[:, :])
            last_(dve.tensor_copy(tile_row[:, :], jump_sum[:, :]))
            split_low(SPLIT_EARLY, E)

        @block.tensor
        def _(pe):
            pe.wait_ge(weights_in, 32)
            for m in range(DC):
                for c in range(DC):
                    last = pe.matmul(act_bank[:, 0, m * D:(m + 1) * D], wv_sb[:, c, m * P:(m + 1) * P],
                                     wo_sb[:, c, :], start=(c == 0), stop=(c == DC - 1))
            last.then_inc(setup_mm, 1)
            pe.wait_ge(setup_chain, 3)
            for c in range(DC):
                last = pe.matmul(dve_bank[:, 0, 0:D], bv_wide[:, c, :], wo_sb[:, c, :],
                                 start=(c == 0), stop=(c == DC - 1))
            last.then_inc(setup_mm, 1)
            pe.sem_inc(probs_used, 3)
            pe.wait_ge(band_in, 16)
            pe.wait_ge(mix_ready, 1)
            pe.wait_ge(rest_in, 48)
            pe.wait_ge(ident_ready, 1)

            def turn(t):
                has_head, has_tail = parts_of(t)

                def act_open(name, k):
                    pe.wait_ge(act_copied, act_free(t, name, k))
                    return act_slot(t, name, k)

                def dve_open(name, k):
                    pe.wait_ge(dve_copied, dve_free(t, name, k))
                    return dve_slot(t, name, k)

                def product(out, stationary, moving):
                    for c in range(DC):
                        last = pe.matmul(out, stationary(c), moving(c), start=(c == 0), stop=(c == DC - 1))
                    return last

                def project(open_, filled, name, weight, src):
                    for k in range(3):
                        bk = open_(name, k)
                        if k < 2:
                            last = product(bk[:, 0:512], lambda c: weight(c, k), lambda c: src[:, c, 0:512])
                        else:
                            for m in range(2):
                                last = product(bk[:, m * 256:(m + 1) * 256], lambda c: weight(c, m),
                                               lambda c: src[:, c, 512:SP_])
                        last.then_inc(filled, 1)

                def transposed(name, src, ready=None):
                    got = 0
                    for k in range(3):
                        bk = act_open(name, k)
                        for j in range(4):
                            c, i = (k, j) if k < 2 else (j // 2, 4 + j % 2)
                            if ready is not None and i + 1 > got:
                                got = i + 1
                                ready(got)
                            last = pe.transpose(bk[:, j * P:(j + 1) * P], src[:, i, c * P:(c + 1) * P], ident[:, :])
                        last.then_inc(act_filled, 1)

                def filtered():
                    pe.wait_ge(x_in, t * 32 + 32)
                    for c in range(DC):
                        bk = act_open("filtered", c)
                        for i in range(4):
                            n = min(BANDW, 512 - i * P)
                            last = pe.matmul(bk[:, i * P:i * P + n], x_sb[:, i, c * P:(c + 1) * P], band[:, 0:n],
                                             start=(i == 0), stop=(i == 3), skip_group_check=True)
                        last.then_inc(act_filled, 1)
                    bk = act_open("filtered", 2)
                    for c in range(DC):
                        o = c * 256
                        pe.matmul(bk[:, o:o + TAPS], x_sb[:, 3, c * P:(c + 1) * P], band[:, P:BANDW],
                                  start=True, stop=False, skip_group_check=True)
                        for i in range(4, 6):
                            n = min(BANDW, SP_ - i * P)
                            a = o + (i - 4) * P
                            last = pe.matmul(bk[:, a:a + n], x_sb[:, i, c * P:(c + 1) * P], band[:, 0:n],
                                             start=False, stop=(i == 5), skip_group_check=True)
                    last.then_inc(act_filled, 1)

                def row_products(name, src, copied, weight, first=None):
                    for k in range(3):
                        bk = dve_open(name, k)
                        if k != 1:
                            pe.wait_ge(act_copied, act_has(t, copied, 1 if k == 0 else 2))
                        for j in range(2):
                            i = 2 * k + j
                            for c in range(DC):
                                last = pe.matmul(bk[:, j * D:(j + 1) * D], src[:, c, i * P:(i + 1) * P], weight[:, c, :],
                                                 start=(c == 0), stop=(c == DC - 1))
                                if (i, c) == (0, 0) and first is not None:
                                    last.then_inc(first, 1)
                        last.then_inc(dve_filled, 1)

                def masked_maxima(n0, n1):
                    for n in range(n0, n1):
                        i, g = divmod(n, MAX_FILLS)
                        c, a = divmod(2 * g, HC)
                        bk = dve_open("max", n)[:, 0:2 * (P + W)]
                        pe.matmul(bk, ident_b[:, :], key_mask[:, min(i, 1), :, :].rearrange("p h k -> p (h k)"),
                                  start=True, stop=False)
                        half, a = divmod(a, HC // 2)
                        rows = slice(half * W, (half + 1) * W)
                        last = pe.matmul(bk.rearrange("p (h k) -> p h k", h=2), qt_r[rows, c, i * P:(i + 1) * P],
                                         k_heads[rows, c, a:a + 2, i * P:i * P + P + W], start=False, stop=True)
                        last.then_inc(dve_filled, 1)

                def maxima_back(half):
                    pe.wait_ge(parts_ready, 2 * t + 1 + half)
                    bk = act_open("maxima", half).bitcast(BF16)
                    pe.sem_inc(pe_passed, 1)
                    i0, i1 = HALVES[half]
                    for i in range(i0, i1):
                        last = pe.transpose(bk[0:3 * H, (i - i0) * P:(i - i0 + 1) * P],
                                            max_parts[:, i, :, :].rearrange("p a h -> p (a h)"), ident_b[:, :])
                        if (half, i) == (1, i0):
                            last.then_inc(maxes_done, 1)
                    last.then_inc(act_filled, 1)

                def scores(n, half):
                    bk = act_open("scores", 2 * n + half).rearrange("p (c a q) -> p c a q", c=DC, a=HC // 2)
                    rows = slice(half * W, (half + 1) * W)
                    pe.matmul(bk, query_mask[:, min(n, 1), :],
                              qmask_and_max[:, :, :].rearrange("p (c f a) s -> p c f a s", c=DC, f=2)[
                                  :, :, half, :, n * W:(n + 1) * W], start=True, stop=False, skip_group_check=True)
                    for c in range(DC):
                        last = pe.matmul(bk[:, c, :, :], kt[rows, c, n * W:n * W + P],
                                         q_heads[rows, c, :, n * W:(n + 1) * W], start=False, stop=(c == DC - 1),
                                         skip_group_check=True)
                    last.then_inc(act_filled, 1)

                def values(n, half):
                    pe.wait_ge(act_copied, act_has(t, "scores", 2 * n + half))
                    if n % 2 == 0 and half == 0:
                        pe.wait_ge(out_copied, t * NT + n // 2 + 1)
                    if has_tail and (n, half) == (2, 0):
                        pe.wait_ge(logits_copied, t)
                    v = v_b[:, n // 2, :, :] if n % 2 == 0 else v_a[:, n // 2, :, :]
                    for c in range(DC):
                        for a in range(HC // 2):
                            g = 2 * c + half
                            q0 = g * P + (n % 2) * W
                            last = pe.matmul(out_bank[32 * a:32 * a + 32, (n // 2) % 2, q0:q0 + W],
                                             v[:, 4 * g + a, :], probs[:, (2 * n + half) % 3, 4 * c + a, :],
                                             start=True, stop=True)
                    return last

                def out_back(i):
                    pe.wait_ge(out_copied, t * NT + i + 1 + 2)
                    bk = dve_open("out", i)
                    for g in range(4):
                        last = pe.transpose(bk[:, g * P:(g + 1) * P], out_t[:, i % 2, g, :], ident[:, :])
                    last.then_inc(dve_filled, 1)

                def route(i):
                    last = product(out_bank[:, 1, i * E:(i + 1) * E], lambda c: xn2t[:, c, i * P:(i + 1) * P],
                                   lambda c: rt_sb[:, c, :])
                    if i == NT - 1:
                        last.then_inc(routed, 1)

                values_bank = [None]

                def project_values(i):
                    if i % 2 == 0:
                        values_bank[0] = act_open("value", i // 2)
                    last = product(values_bank[0][:, i % 2 * D:(i % 2 + 1) * D], lambda c: xnt[:, c, i * P:(i + 1) * P],
                                   lambda c: wqkv_sb[:, c, 2 * D:3 * D])
                    if i % 2 == 1:
                        last.then_inc(act_filled, 1)

                def ranks():
                    bk = dve_open("rank", 0)
                    pe.wait_ge(chosen_ready, t)
                    pe.matmul(bk[:, 0:NT * E], before[:, :], chosen[:, :, :].rearrange("p i e -> p (i e)"),
                              start=True, stop=False, skip_group_check=True)
                    for k in range(1, NT):
                        pe.matmul(bk[:, k * E:NT * E], ones_b[:, :], chosen[:, 0:NT - k, :].rearrange("p i e -> p (i e)"),
                                  start=False, stop=(k == NT - 1), skip_group_check=True)
                    for i in range(NT):
                        last = pe.matmul(bk[:, NT * E:NT * E + E], ones_b[:, :], chosen[:, i, :],
                                         start=False, stop=(i == NT - 1), skip_group_check=True)
                    last.then_inc(dve_filled, 1)

                if has_head:
                    filtered()
                    row_products("h", st, "filtered", mix_w, conv_done)
                if has_tail:
                    pe.wait_ge(dve_copied, dve_has_out_of_last(t))
                    transposed("attn_t", attn_rows)
                    row_products("proj", attn_t, "attn_t", wout_sb)
                if has_head:
                    transposed("xn_t", xn, lambda n: pe.wait_ge(xn_ready[0], t * NT + n))
                    pe.wait_ge(act_copied, act_has(t, "xn_t", 2))
                    project(dve_open, dve_filled, "key", lambda c, m: wqkv_sb[:, c, D + m * P:D + (m + 1) * P], xnt)
                    project(act_open, act_filled, "query", lambda c, m: wqkv_sb[:, c, m * P:(m + 1) * P], xnt)
                if has_tail:
                    transposed("xn2_t", xn2_cols, lambda n: pe.wait_ge(xn_ready[1], (t - 1) * NT + n))
                    pe.wait_ge(act_copied, act_has(t, "xn2_t", 2))
                if not has_head:
                    for i in range(NT):
                        route(i)
                    ranks()
                    return
                if not has_tail:
                    pe.wait_ge(max_consts, 2)
                project_values(0)
                project_values(1)
                pe.wait_ge(k_placed, (t + 1) * N_PLACE)
                pe.wait_ge(act_copied, act_has(t, "query", 2))
                between = [lambda i=i: project_values(i) for i in range(2, NT)]
                if has_tail:
                    between += [lambda i=i: route(i) for i in range(NT)]
                first = HALVES[0][1] * MAX_FILLS + RING
                for n in range(NT * MAX_FILLS):
                    while between and BETWEEN_AT[-len(between) if has_tail else -len(between) - NT] == n:
                        between.pop(0)()
                    if n == first:
                        maxima_back(0)
                    masked_maxima(n, n + 1)
                pe.wait_ge(q_placed, (t + 1) * N_PLACE)
                pe.wait_ge(max_placed[0], (t + 1) * 48)
                if not has_tail:
                    pe.wait_ge(consts_ready, N_CONSTS)
                for m in range(2 * NB + 2):
                    if m == MAX_LATE:
                        maxima_back(1)
                    if m == 4 * HALVES[0][1]:
                        pe.wait_ge(max_placed[1], (t + 1) * 48)
                    if m < 2 * NB:
                        scores(*divmod(m, 2))
                    if m == 2:
                        pe.wait_ge(v_shifted, (t + 1) * 32)
                    if m >= 2:
                        n, half = divmod(m - 2, 2)
                        last = values(n, half)
                        last.then_inc(probs_used, 1)
                        if n % 2 == 1 and half == 0 and n >= 3:
                            i = n // 2 - 1
                            if has_tail and i == RANK_AFTER:
                                ranks()
                            out_back(i)
                out_back(NT - 1)

            def dve_has_out_of_last(t):
                return fills_of(DVE_ORDER, DVE_HEAD, t)[1] + RING

            turn(0)
            with pe.Fori(1, B) as t:
                turn(t)
            turn(B)


def experts(nc, x_slots, sums, shared, w_in_loaded, rest_loaded, w_split, tile_expert, tile_row, tile_after, out):
    with ExitStack() as ctx:
        def sb(name, shape, dt=F32):
            return ctx.enter_context(nc.sbuf_tensor(name, shape, dt))

        def sem(name):
            return ctx.enter_context(nc.semaphore(name))

        in_bank = ctx.enter_context(nc.psum_tensor("in_bank", [P, 2, 512], F32))
        row_bank = ctx.enter_context(nc.psum_tensor("row_bank", [P, 2, 512], F32))
        turn_bank = ctx.enter_context(nc.psum_tensor("turn_bank", [P, 2, 512], F32))
        y_bank = ctx.enter_context(nc.psum_tensor("y_bank", [P, 2, 512], F32))

        ident = sb("ident2", [P, P])
        w_high, w_low, w_out_sb = shared["w_high"], shared["w_low"], shared["w_out"]
        b_in_sb = shared["b_in"].rearrange("p (e n) -> p e n", e=E)
        b_out_sb = shared["b_out"].rearrange("p (e n) -> p e n", e=E)
        rows = sb("rows", [P, UNROLL, ROW])
        rows_high = sb("rows_high", [P, 2, DC, P], F32R)
        rows_low = sb("rows_low", [P, 2, DC, P], F32R)
        hid = sb("hid", [P, 2, 2 * I])
        act_g = sb("act_g", [P, 2, I])
        prod = sb("prod", [P, 2, I])
        prod_t = sb("prod_t", [P, 2, DC, P])
        y = sb("y", [P, Y_BUFS, D])

        ident_ready = sem("ident_ready")
        ones_ready = sem("ones_ready")
        rows_in = [sem(f"rows_in_{k}") for k in range(UNROLL)]
        rows_turned = sem("rows_turned")
        rows_high_ready = sem("rows_high_ready")
        rows_low_ready = sem("rows_low_ready")
        hid_filled = sem("hid_filled")
        hid_ready = sem("hid_ready")
        gated = sem("gated")
        prod_ready = sem("prod_ready")
        turned = sem("turned")
        prod_t_ready = sem("prod_t_ready")
        summed = sem("summed")
        y_ready = sem("y_ready")
        added = [sem(f"added_{k}") for k in range(UNROLL)]
        tiles_added = sem("tiles_added")
        passed = sem("passed")
        out_saved = sem("out_saved")

        def expert_of(eng, t):
            return eng.value_load(tile_expert[0:1, bass.ds(t, 1)], min_val=0, max_val=E - 1)

        def row_of(eng, t):
            return eng.value_load(tile_row[0:1, bass.ds(t, 1)], min_val=0, max_val=E * REGION + (MORE - 1) * P)

        def gate(k8):
            return rows[:, k8, D:D + 1]

        block = ctx.enter_context(nc.Block())

        @block.sync
        def _(sp):
            def load(t, k):
                sp.dma_start(rows[:, k, :], x_slots[bass.ds(row_of(sp, t), P), :]).then_inc(rows_in[k], 16)

            for k in range(UNROLL):
                load(k, k)
            sp.sem_inc(tiles_added, 1)
            with sp.Fori(0, TILES // UNROLL - 1) as j:
                for k in range(UNROLL):
                    sp.wait_ge(added[k], j * 16 + 16)
                    sp.sem_inc(tiles_added, 1)
                    load(j * UNROLL + UNROLL + k, k)
            for k in range(UNROLL):
                sp.wait_ge(added[k], TILES // UNROLL * 16)
                sp.sem_inc(tiles_added, 1)
            most = S // 16 * 16
            for b in range(B):
                sp.dma_start(out[b, 0:most, :].rearrange("(g r) d -> g (r d)", g=16),
                             sums[b * SP_:b * SP_ + most, :].rearrange("(g r) d -> g (r d)", g=16)).then_inc(out_saved, 16)
            sp.dma_start(out[:, most:S, :],
                         sums[0:ROWS, :].rearrange("(b s) d -> b s d", b=B)[:, most:S, :]).then_inc(out_saved, 16)
            sp.wait_ge(out_saved, (B + 1) * 16)

        @block.gpsimd
        def _(pool):
            pool.memset(ident[:, :], 1.0).then_inc(ones_ready, 1)
            pool.wait_ge(ones_ready, 1)
            pool.affine_select(ident[:, :], ident[:, :], [[-1, P]], ALU.is_equal, 0.0, base=0,
                               channel_multiplier=1).then_inc(ident_ready, 1)

            with pool.Fori(0, TILES // UNROLL) as j:
                for k in range(UNROLL):
                    t = j * UNROLL + k
                    after = pool.value_load(tile_after[0:1, bass.ds(t, 1)], min_val=1, max_val=TILES + 1)
                    pool.wait_ge(y_ready, t + 1)
                    pool.wait_ge(tiles_added, after)
                    pool.sem_inc(passed, 1)
                    pool.indirect_dma_start(
                        out=sums, out_offset=bass.IndirectOffsetOnAxis(ap=rows[:, k, D + 1:D + 2].bitcast(mybir.dt.uint32), axis=0),
                        in_=y[:, k % Y_BUFS, :], in_offset=None, compute_op=ALU.add).then_inc(added[k], 16)

        @block.scalar
        def _(act):
            def turn_rows(t, k):
                act.wait_ge(rows_turned, t + 1)
                act.copy(rows_high[:, k % 2, :, :],
                         row_bank[:, k % 2, 0:256].rearrange("p (c n) -> p c n", c=2)).then_inc(rows_high_ready, 1)

            turn_rows(0, 0)
            turn_rows(1, 1)

            def step(t, k, more=True):
                act.wait_ge(hid_ready, t + 1)
                act.activation(act_g[:, k % 2, :], hid[:, k % 2, 0:I], ACT.Silu).then_inc(gated, 1)
                if more:
                    turn_rows(t + 2, k)
                act.wait_ge(turned, t + 1)
                act.copy(prod_t[:, k % 2, :, :],
                         turn_bank[:, k % 2, 0:256].rearrange("p (c n) -> p c n", c=2)).then_inc(prod_t_ready, 1)

            act.preload_act_table(ACT.Silu)
            with act.Fori(0, TILES // UNROLL - 1) as j:
                for k in range(UNROLL):
                    step(j * UNROLL + k, k)
            for k in range(UNROLL):
                step(TILES - UNROLL + k, k, more=(k < UNROLL - 2))

        @block.vector
        def _(dve):
            dve.wait_ge(rest_loaded, 48)

            numbers = {}

            def add_b_in(t, k):
                numbers[k] = e = expert_of(dve, t)
                dve.wait_ge(hid_filled, t + 1)
                dve.tensor_tensor(hid[:, k % 2, :], in_bank[:, k % 2, :], b_in_sb[:, bass.ds(e, 1), :],
                                  ALU.add).then_inc(hid_ready, 1)

            def low_rows(t, k):
                dve.wait_ge(rows_high_ready, t + 1)
                dve.tensor_tensor(rows_low[:, k % 2, :, :], row_bank[:, k % 2, 0:256].rearrange("p (c n) -> p c n", c=2),
                                  rows_high[:, k % 2, :, :], ALU.subtract).then_inc(rows_low_ready, 1)

            def gate_rows(t, k):
                dve.wait_ge(gated, t + 1)
                dve.scalar_tensor_tensor(prod[:, k % 2, :], act_g[:, k % 2, :], gate(k), hid[:, k % 2, I:2 * I],
                                         ALU.mult, ALU.mult).then_inc(prod_ready, 1)

            def results(t, k, y_saved, e):
                dve.wait_ge(summed, t + 1)
                if y_saved is not None:
                    dve.wait_ge(added[(k + UNROLL - Y_BUFS) % UNROLL], y_saved)
                dve.sem_inc(passed, 1)
                dve.scalar_tensor_tensor(y[:, k % Y_BUFS, :], b_out_sb[:, bass.ds(e, 1), :].rearrange("p e n -> p (e n)"),
                                         gate(k), y_bank[:, k % 2, 0:D], ALU.mult, ALU.add).then_inc(y_ready, 1)

            def step(t, k, y_saved=None, first=False, more=2):
                if k == 0:
                    numbers.clear()
                gate_rows(t, k)
                if more >= 2:
                    low_rows(t + 2, k)
                if more >= 1:
                    add_b_in(t + 1, k + 1)
                if k == 0 and not first:
                    numbers[-1] = expert_of(dve, t - 1)
                if k == 1:
                    numbers[0] = expert_of(dve, t - 1)
                if not first:
                    results(t - 1, (k - 1) % UNROLL, y_saved, numbers[k - 1])

            low_rows(0, 0)
            low_rows(1, 1)
            add_b_in(0, 0)
            for k in range(UNROLL):
                step(k, k, 16 if k > Y_BUFS else None, first=(k == 0))
            with dve.Fori(1, TILES // UNROLL - 1) as j:
                for k in range(UNROLL):
                    step(j * UNROLL + k, k, (j + (k > Y_BUFS)) * 16 if k else j * 16)
            last_j = TILES // UNROLL - 1
            for k in range(UNROLL):
                step(TILES - UNROLL + k, k, (last_j + (k > Y_BUFS)) * 16, more=min(UNROLL - 1 - k, 2))
            results(TILES - 1, UNROLL - 1, (last_j + 1) * 16, numbers[UNROLL - 1])

        @block.tensor
        def _(pe):
            pe.wait_ge(w_split, E)
            pe.wait_ge(rest_loaded, 48)
            pe.wait_ge(ident_ready, 1)

            def turn_rows(t, k, arrivals):
                pe.wait_ge(rows_in[k], arrivals)
                for c in range(DC):
                    last = pe.transpose(row_bank[:, k % 2, c * P:(c + 1) * P], rows[:, k, c * P:(c + 1) * P], ident[:, :])
                last.then_inc(rows_turned, 1)

            numbers = {}

            def widen(t, k):
                if k not in numbers:
                    numbers[k] = expert_of(pe, t)
                e = numbers[k]
                pe.wait_ge(rows_low_ready, t + 1)
                parts = [(r, w, c) for c in range(DC)
                         for r, w in ((rows_high, w_high), (rows_high, w_low), (rows_low, w_high))]
                for n, (r, w, c) in enumerate(parts):
                    last = pe.matmul(in_bank[:, k % 2, :], r[:, k % 2, c, :], w[:, c, bass.ds(e, 1), :],
                                     start=(n == 0), stop=(n == len(parts) - 1))
                last.then_inc(hid_filled, 1)

            def narrow(t, k, e):
                pe.wait_ge(prod_t_ready, t + 1)
                for c in range(DC):
                    last = pe.matmul(y_bank[:, k % 2, 0:D], prod_t[:, k % 2, c, :], w_out_sb[:, c, bass.ds(e, 1), :],
                                     start=(c == 0), stop=(c == DC - 1))
                last.then_inc(summed, 1)

            def step(t, k, arrivals, more, first=False):
                if k == 0:
                    numbers.clear()
                if more >= 2:
                    turn_rows(t + 2, (k + 2) % UNROLL, arrivals)
                if more >= 1:
                    widen(t + 1, k + 1)
                if k == 0 and not first:
                    numbers[-1] = expert_of(pe, t - 1)
                if k == 1:
                    numbers[0] = expert_of(pe, t - 1)
                pe.wait_ge(prod_ready, t + 1)
                for c in range(DC):
                    last = pe.transpose(turn_bank[:, k % 2, c * P:(c + 1) * P], prod[:, k % 2, c * P:(c + 1) * P], ident[:, :])
                last.then_inc(turned, 1)
                if not first:
                    narrow(t - 1, k - 1, numbers[k - 1])

            turn_rows(0, 0, 16)
            turn_rows(1, 1, 16)
            widen(0, 0)
            for k in range(UNROLL):
                step(k, k, (1 + (k >= UNROLL - 2)) * 16, 2, first=(k == 0))
            with pe.Fori(1, TILES // UNROLL - 1) as j:
                for k in range(UNROLL):
                    step(j * UNROLL + k, k, (j + 1 + (k >= UNROLL - 2)) * 16, 2)
            last_j = TILES // UNROLL - 1
            for k in range(UNROLL):
                step(last_j * UNROLL + k, k, (last_j + 1) * 16, min(UNROLL - 1 - k, 2))
            narrow(TILES - 1, UNROLL - 1, numbers[UNROLL - 1])


def build(nc, x, wv, bv, wo_t, bo, decay_rev, w_qkv, w_out, router_t, w_in_t, b_in, w_out_t, b_out, out):
    band_dram = nc.dram_tensor("band_dram", (P * 161 + 161,), F32, kind="Internal").ap()
    sums = nc.dram_tensor("sums", (ROWS + (MORE + 1) * P, D), F32, kind="Internal").ap()
    x_slots = nc.dram_tensor("x_slots", (E * REGION + MORE * P, ROW), F32, kind="Internal").ap()
    with ExitStack() as ctx:
        def sb(name, shape, dt=F32):
            return ctx.enter_context(nc.sbuf_tensor(name, shape, dt))

        tile_expert = sb("tile_expert", [1, TILES], mybir.dt.int32)
        tile_row = sb("tile_row", [1, TILES], mybir.dt.int32)
        tile_after = sb("tile_after", [1, TILES], mybir.dt.int32)
        w_in_loaded = ctx.enter_context(nc.semaphore("w_in_loaded"))
        rest_loaded = ctx.enter_context(nc.semaphore("rest_loaded"))
        w_split = ctx.enter_context(nc.semaphore("w_split"))
        n_q, n_v, n_x, n_k = DC * HC // 2 * SP_, NT * H * 2 * HD, NT * D, DC * HC // 2 * KP
        with nc.sbuf_tensor("w_in_low", [P, n_q + n_v], F32R) as w_in_low:
            pass
        q_and_v = sb("q_and_v", [P, n_q + n_v])
        n_in = DC * E * 2 * I
        with nc.sbuf_tensor("w_in_high", [P, n_in], F32R) as w_in_high:
            pass
        qmask_and_max = sb("qmask_and_max", [W + 3, H, SP_], BF16)
        v_b = sb("v_b", [P, NT, H, 2 * HD])
        assert 4 * n_in <= 2 * H * SP_ + 4 * n_v
        x_h_xn = sb("x_h_xn", [P, 3 * n_x])
        with nc.sbuf_tensor("keys", [P, n_k], F32R) as keys:
            pass
        biases = sb("biases", [P, n_k])
        n_out = DC * E * D
        assert n_in <= n_q + n_v and n_out <= 3 * n_x and E * (2 * I + D) <= n_k
        shared = {
            "q_heads": q_and_v[:, 0:n_q].rearrange("p (c a s) -> p c a s", c=DC, a=HC // 2),
            "v_a": q_and_v[:, n_q:].rearrange("p (i h d) -> p i h d", i=NT, h=H),
            "x": x_h_xn[:, 0:n_x].rearrange("p (i d) -> p i d", i=NT),
            "h": x_h_xn[:, n_x:2 * n_x].rearrange("p (i d) -> p i d", i=NT),
            "xn": x_h_xn[:, 2 * n_x:3 * n_x].rearrange("p (i d) -> p i d", i=NT),
            "k_heads": keys[:, :].rearrange("p (c a s) -> p c a s", c=DC, a=HC // 2),
            "w_in": q_and_v[:, 0:n_in].rearrange("p (c e n) -> p c e n", c=DC, e=E),
            "w_high": w_in_high[:, :].rearrange("p (c e n) -> p c e n", c=DC, e=E),
            "w_low": w_in_low[:, 0:n_in].rearrange("p (c e n) -> p c e n", c=DC, e=E),
            "qmask_and_max": qmask_and_max[:, :, :],
            "v_b": v_b[:, :, :, :],
            "w_out": x_h_xn[:, 0:n_out].rearrange("p (c e n) -> p c e n", c=DC, e=E),
            "b_in": biases[:, 0:E * 2 * I],
            "b_out": biases[:, E * 2 * I:E * (2 * I + D)],
        }
        token_mixer_and_attention(nc, x, wv, bv, wo_t, bo, decay_rev, w_qkv, w_out, router_t,
                                  w_in_t, b_in, w_out_t, b_out, band_dram, sums, x_slots, shared, w_in_loaded, rest_loaded, w_split,
                                  tile_expert, tile_row, tile_after)
        experts(nc, x_slots, sums, shared, w_in_loaded, rest_loaded, w_split, tile_expert, tile_row, tile_after, out)


def kernel(x, L0_tok_Wv, L0_tok_bv, L0_tok_Wo, L0_tok_bo, L0_tok_decay_w, L0_attn_W_qkv, L0_attn_W_out,
           L0_ffn_router_w, L0_ffn_w_in, L0_ffn_b_in, L0_ffn_w_out, L0_ffn_b_out):
    import numpy as np
    import concourse.bacc as bacc
    from concourse.bass_utils import run_bass_kernel_spmd

    laid_out = {
        "x": x, "wv": L0_tok_Wv, "bv": np.asarray(L0_tok_bv).reshape(DC, P).T, "wo_t": np.asarray(L0_tok_Wo).T, "bo": L0_tok_bo,
        "decay_rev": np.asarray(L0_tok_decay_w)[::-1], "w_qkv": L0_attn_W_qkv, "w_out": L0_attn_W_out,
        "router_t": np.asarray(L0_ffn_router_w).T,
        "w_in_t": np.asarray(L0_ffn_w_in).transpose(2, 0, 1), "b_in": L0_ffn_b_in,
        "w_out_t": np.asarray(L0_ffn_w_out).transpose(2, 0, 1), "b_out": L0_ffn_b_out,
    }
    nc = bacc.Bacc("TRN2", target_bir_lowering=False, num_devices=1)
    arrays, args = {}, []
    for name, a in laid_out.items():
        a = np.ascontiguousarray(a)
        arrays[f"in_{name}"] = a
        args.append(nc.dram_tensor(f"in_{name}", a.shape, mybir.dt.from_np(a.dtype), kind="ExternalInput").ap())
    out = nc.dram_tensor("out", (B, S, D), F32, kind="ExternalOutput").ap()
    build(nc, *args, out)
    r = run_bass_kernel_spmd(nc, [arrays], core_ids=[0])
    return r.results[0]["out"]
```
